# Optimizing a Trainium2 kernel written in Bass

```python
import numpy as np
import jax
import jax.numpy as jnp

def _softmax(x, axis=-1):
    return jax.nn.softmax(x, axis=axis)

def _gelu(x):
    return jax.nn.gelu(x, approximate=True)

def _silu(x):
    return jax.nn.silu(x)

def _sigmoid(x):
    return jax.nn.sigmoid(x)

def _layernorm(x, axis=-1, eps=1e-05):
    m = jnp.mean(x, axis=axis, keepdims=True)
    v = jnp.var(x, axis=axis, keepdims=True)
    return (x - m) / jnp.sqrt(v + eps)

def _scatter_add(tgt, idx, src, axis=0):
    return tgt.at[idx].add(src)

def _segment_sum(src, seg, n):
    return jax.ops.segment_sum(src, seg, n)
kernel_name = 'mk_gnn_preln_d4_gnn_r8_75f967'

def setup_inputs(seed: int=0):
    np.random.seed(seed)
    _w = jnp.asarray

    def _rec_inputs():
        import jax
        import jax.numpy as jnp
        _gk = jax.random.key(seed)
        x = -0.000202 + 1 * jax.random.normal(jax.random.fold_in(_gk, 1), (12500, 128), jnp.float32)
        src = jax.random.randint(jax.random.fold_in(_gk, 2), (200000,), 0, 12500, jnp.int32)
        dst = jnp.minimum((12500 * jax.random.uniform(jax.random.fold_in(_gk, 3), (200000,)) ** 2.0).astype(jnp.int32), 99999)
        _o = jnp.argsort(dst, stable=True)
        src = src[_o]
        dst = dst[_o]
        edge_attr_16 = 5.96457e-05 + 0.999887 * jax.random.normal(jax.random.fold_in(_gk, 12), (200000, 16), jnp.float32)
        edge_attr_6 = 0.00011001 + 1.00018 * jax.random.normal(jax.random.fold_in(_gk, 13), (200000, 6), jnp.float32)
        edge_type_8 = jax.random.randint(jax.random.fold_in(_gk, 16), (200000,), 0, 8, jnp.int32)
        return (x, src, dst, edge_attr_16, edge_attr_6, edge_type_8)
    x, src, dst, edge_attr_16, edge_attr_6, edge_type_8 = _rec_inputs()

    def _L0_gnn_setup():
        import jax, jax.numpy as jnp
        import numpy as np
        N, IN, H, D = (6250, 128, 4, 32)
        HID = H * D
        E = 100000
        key = jax.random.key(seed)
        ks = jax.random.split(key, 16)
        s_in = 1.0 / np.sqrt(IN)
        s_g = 1.0 / np.sqrt(3 * HID)
        inp = {'feat': jax.random.normal(ks[0], (N, IN), jnp.float32), 'src': jax.random.randint(ks[1], (E,), 0, N, jnp.int32), 'dst': jax.random.randint(ks[2], (E,), 0, N, jnp.int32), 'Wq': jax.random.normal(ks[3], (IN, HID), jnp.float32) * s_in, 'bq': jnp.zeros((HID,), jnp.float32), 'Wk': jax.random.normal(ks[4], (IN, HID), jnp.float32) * s_in, 'bk': jnp.zeros((HID,), jnp.float32), 'Wv': jax.random.normal(ks[5], (IN, HID), jnp.float32) * s_in, 'bv': jnp.zeros((HID,), jnp.float32), 'Ws': jax.random.normal(ks[6], (IN, HID), jnp.float32) * s_in, 'bs': jnp.zeros((HID,), jnp.float32), 'Wg': jax.random.normal(ks[7], (3 * HID, 1), jnp.float32) * s_g, 'bg': jnp.zeros((1,), jnp.float32), 'gamma': jnp.ones((HID,), jnp.float32), 'beta': jnp.zeros((HID,), jnp.float32), 'alpha': jnp.asarray(0.25, jnp.float32)}
        return inp
    _L0_gnn_all = _L0_gnn_setup()
    _L0_gnn_in = {k: v for k, v in _L0_gnn_all.items() if k in ('Wq', 'bq', 'Wk', 'bk', 'Wv', 'bv', 'Ws', 'bs', 'Wg', 'bg', 'gamma', 'beta', 'alpha')}
    del _L0_gnn_all

    def _L1_gnn_setup():
        import jax, jax.numpy as jnp
        import numpy as np
        N, E, IN_DIM, OUT_DIM, R = (6250, 100000, 128, 128, 8)
        key = jax.random.key(seed)
        k1, k2, k3, k4, k5 = jax.random.split(key, 5)
        x = jax.random.normal(k1, (N, IN_DIM), dtype=jnp.float32)
        edge_index = jax.random.randint(k2, (2, E), 0, N, dtype=jnp.int32)
        edge_type = jax.random.randint(k3, (E,), 0, R, dtype=jnp.int32)
        lim_w = float(np.sqrt(6.0 / (IN_DIM + OUT_DIM)))
        weight = jax.random.uniform(k4, (R, IN_DIM, OUT_DIM), dtype=jnp.float32, minval=-lim_w, maxval=lim_w)
        self_weight = jax.random.uniform(k5, (IN_DIM, OUT_DIM), dtype=jnp.float32, minval=-lim_w, maxval=lim_w)
        return {'x': x, 'weight': weight, 'self_weight': self_weight, 'edge_index': edge_index, 'edge_type': edge_type}
    _L1_gnn_all = _L1_gnn_setup()
    _L1_gnn_in = {k: v for k, v in _L1_gnn_all.items() if k in ('weight', 'self_weight')}
    del _L1_gnn_all

    def _L2_gnn_setup():
        import jax, jax.numpy as jnp
        import numpy as np
        N, E, D_EDGE, H = (6250, 80000, 16, 128)
        BN_EPS = 1e-05
        key = jax.random.key(seed)
        ks = jax.random.split(key, 8)
        return {'x': jax.random.normal(ks[0], (N, H), jnp.float32), 'edge_attr': jax.random.normal(ks[1], (E, D_EDGE), jnp.float32), 'W_edge': jax.random.normal(ks[2], (D_EDGE, H), jnp.float32) * (1.0 / np.sqrt(D_EDGE)), 'b_edge': jnp.zeros((H,), jnp.float32), 'W1': jax.random.normal(ks[3], (H, 2 * H), jnp.float32) * (1.0 / np.sqrt(H)), 'b1': jnp.zeros((2 * H,), jnp.float32), 'gamma': jnp.ones((2 * H,), jnp.float32), 'beta': jnp.zeros((2 * H,), jnp.float32), 'W2': jax.random.normal(ks[4], (2 * H, H), jnp.float32) * (1.0 / np.sqrt(2 * H)), 'b2': jnp.zeros((H,), jnp.float32), 'edge_index': jax.random.randint(ks[5], (2, E), 0, N, jnp.int64), 'self_loop_index': 0, 'self_loop_type': 4}
    _L2_gnn_all = _L2_gnn_setup()
    _L2_gnn_in = {k: v for k, v in _L2_gnn_all.items() if k in ('W_edge', 'b_edge', 'W1', 'b1', 'gamma', 'beta', 'W2', 'b2')}
    del _L2_gnn_all

    def _L3_gnn_setup():
        import jax, jax.numpy as jnp
        import numpy as np
        N_NODES = 6250
        N_EDGES = 100000
        IN_F = 128
        OUT_F = 128
        EDGE_F = 6
        key = jax.random.key(seed)
        k1, k2, k3, k4, k5, k6, k7 = jax.random.split(key, 7)
        nodeFeatures = jax.random.normal(k1, (N_NODES, IN_F), dtype=jnp.float32)
        edgeIndex = jax.random.randint(k2, (N_EDGES, 2), 0, N_NODES, dtype=jnp.int64)
        edgeFeatures = jax.random.normal(k3, (N_EDGES, EDGE_F), dtype=jnp.float32)
        lim_n = 1.0 / np.sqrt(IN_F)
        lim_e = 1.0 / np.sqrt(EDGE_F)
        W = jax.random.uniform(k4, (IN_F, OUT_F), minval=-lim_n, maxval=lim_n, dtype=jnp.float32)
        b = jax.random.uniform(k5, (OUT_F,), minval=-lim_n, maxval=lim_n, dtype=jnp.float32)
        We = jax.random.uniform(k6, (EDGE_F, OUT_F), minval=-lim_e, maxval=lim_e, dtype=jnp.float32)
        be = jax.random.uniform(k7, (OUT_F,), minval=-lim_e, maxval=lim_e, dtype=jnp.float32)
        return {'nodeFeatures': nodeFeatures, 'edgeIndex': edgeIndex, 'edgeFeatures': edgeFeatures, 'W': W, 'b': b, 'We': We, 'be': be}
    _L3_gnn_all = _L3_gnn_setup()
    _L3_gnn_in = {k: v for k, v in _L3_gnn_all.items() if k in ('W', 'b', 'We', 'be')}
    del _L3_gnn_all
    return {'x': x, 'src': src, 'dst': dst, 'edge_attr_16': edge_attr_16, 'edge_attr_6': edge_attr_6, 'edge_type_8': edge_type_8, 'L0_gnn_Wq': _L0_gnn_in['Wq'], 'L0_gnn_bq': _L0_gnn_in['bq'], 'L0_gnn_Wk': _L0_gnn_in['Wk'], 'L0_gnn_bk': _L0_gnn_in['bk'], 'L0_gnn_Wv': _L0_gnn_in['Wv'], 'L0_gnn_bv': _L0_gnn_in['bv'], 'L0_gnn_Ws': _L0_gnn_in['Ws'], 'L0_gnn_bs': _L0_gnn_in['bs'], 'L0_gnn_Wg': _L0_gnn_in['Wg'], 'L0_gnn_bg': _L0_gnn_in['bg'], 'L0_gnn_gamma': _L0_gnn_in['gamma'], 'L0_gnn_beta': _L0_gnn_in['beta'], 'L0_gnn_alpha': _L0_gnn_in['alpha'], 'L1_gnn_weight': _L1_gnn_in['weight'], 'L1_gnn_self_weight': _L1_gnn_in['self_weight'], 'L2_gnn_W_edge': _L2_gnn_in['W_edge'], 'L2_gnn_b_edge': _L2_gnn_in['b_edge'], 'L2_gnn_W1': _L2_gnn_in['W1'], 'L2_gnn_b1': _L2_gnn_in['b1'], 'L2_gnn_gamma': _L2_gnn_in['gamma'], 'L2_gnn_beta': _L2_gnn_in['beta'], 'L2_gnn_W2': _L2_gnn_in['W2'], 'L2_gnn_b2': _L2_gnn_in['b2'], 'L3_gnn_W': _L3_gnn_in['W'], 'L3_gnn_b': _L3_gnn_in['b'], 'L3_gnn_We': _L3_gnn_in['We'], 'L3_gnn_be': _L3_gnn_in['be']}

def reference(x, src, dst, edge_attr_16, edge_attr_6, edge_type_8, L0_gnn_Wq, L0_gnn_bq, L0_gnn_Wk, L0_gnn_bk, L0_gnn_Wv, L0_gnn_bv, L0_gnn_Ws, L0_gnn_bs, L0_gnn_Wg, L0_gnn_bg, L0_gnn_gamma, L0_gnn_beta, L0_gnn_alpha, L1_gnn_weight, L1_gnn_self_weight, L2_gnn_W_edge, L2_gnn_b_edge, L2_gnn_W1, L2_gnn_b1, L2_gnn_gamma, L2_gnn_beta, L2_gnn_W2, L2_gnn_b2, L3_gnn_W, L3_gnn_b, L3_gnn_We, L3_gnn_be):
    import jax
    import jax.numpy as jnp

    def _L0_gnn_ref(feat, src, dst, Wq, bq, Wk, bk, Wv, bv, Ws, bs, Wg, bg, gamma, beta, alpha):
        import jax, jax.numpy as jnp
        import numpy as np
        N, IN, H, D = (6250, 128, 4, 32)
        HID = H * D
        E = 100000
        n = feat.shape[0]
        q = (feat @ Wq + bq).reshape(n, H, D)
        k = (feat @ Wk + bk).reshape(n, H, D)
        v = (feat @ Wv + bv).reshape(n, H, D)
        a = jnp.einsum('ehd,ehd->eh', q[src], k[dst]) / jnp.sqrt(jnp.float32(D))
        m = jax.ops.segment_max(a, dst, num_segments=n)
        m = jax.lax.stop_gradient(jnp.where(jnp.isfinite(m), m, 0.0))
        ex = jnp.exp(a - m[dst])
        denom = jax.ops.segment_sum(ex, dst, num_segments=n)
        denom = jnp.where(denom > 0, denom, 1.0)
        sa = ex / denom[dst]
        msg = v[src] * sa[:, :, None]
        agg = jax.ops.segment_sum(msg, dst, num_segments=n).reshape(n, HID)
        skip = feat @ Ws + bs
        g = jax.nn.sigmoid(jnp.concatenate([skip, agg, skip - agg], axis=-1) @ Wg + bg)
        rst = g * skip + (1.0 - g) * agg
        mu = rst.mean(-1, keepdims=True)
        var = rst.var(-1, keepdims=True)
        rst = (rst - mu) * jax.lax.rsqrt(var + 1e-05) * gamma + beta
        rst = jnp.where(rst >= 0, rst, alpha * rst)
        return rst

    def _L1_gnn_ref(x, weight, self_weight, edge_index, edge_type):
        import jax, jax.numpy as jnp
        import numpy as np
        N, E, IN_DIM, OUT_DIM, R = (6250, 100000, 128, 128, 8)
        n = x.shape[0]
        r = weight.shape[0]
        d_out = weight.shape[2]
        src, dst = (edge_index[0], edge_index[1])
        src_all = jnp.concatenate([src, dst])
        dst_all = jnp.concatenate([dst, src])
        et_all = jnp.concatenate([edge_type, edge_type])
        xw = jnp.einsum('ni,rio->rno', x, weight)
        msg = xw[et_all, src_all]
        seg = et_all.astype(jnp.int32) * n + dst_all
        agg = jax.ops.segment_sum(msg, seg, num_segments=r * n).reshape(r, n, d_out)
        deg = jax.ops.segment_sum(jnp.ones_like(seg, dtype=x.dtype), seg, num_segments=r * n).reshape(r, n)
        deg_inv = jnp.where(deg > 0, 1.0 / jnp.maximum(deg, 1.0), jnp.zeros_like(deg))
        out = jnp.sum(agg * deg_inv[..., None], axis=0)
        out = out + x @ self_weight
        return out

    def _L2_gnn_ref(x, edge_attr, W_edge, b_edge, W1, b1, gamma, beta, W2, b2, edge_index, self_loop_index, self_loop_type):
        import jax, jax.numpy as jnp
        import numpy as np
        N, E, D_EDGE, H = (6250, 80000, 16, 128)
        BN_EPS = 1e-05
        n = x.shape[0]
        loops = jnp.arange(n, dtype=edge_index.dtype)
        ei = jnp.concatenate([edge_index, jnp.stack([loops, loops])], axis=1)
        sl_attr = jnp.zeros((n, edge_attr.shape[1]), edge_attr.dtype)
        sl_attr = sl_attr.at[:, self_loop_index].set(jnp.asarray(self_loop_type, edge_attr.dtype))
        ea = jnp.concatenate([edge_attr, sl_attr], axis=0)
        edge_emb = ea @ W_edge + b_edge
        h = x[ei[1]] + edge_emb
        agg = jax.ops.segment_sum(h, ei[0], num_segments=n)
        h1 = agg @ W1 + b1
        mean = jnp.mean(h1, axis=0)
        var = jnp.mean(jnp.square(h1 - mean), axis=0)
        h1 = gamma * (h1 - mean) * jax.lax.rsqrt(var + BN_EPS) + beta
        h1 = jax.nn.relu(h1)
        return h1 @ W2 + b2

    def _L3_gnn_ref(nodeFeatures, edgeIndex, edgeFeatures, W, b, We, be):
        import jax, jax.numpy as jnp
        import numpy as np
        N_NODES = 6250
        N_EDGES = 100000
        IN_F = 128
        OUT_F = 128
        EDGE_F = 6
        transformed = nodeFeatures @ W + b
        edgeMsg = edgeFeatures @ We + be
        src = edgeIndex[:, 0]
        dst = edgeIndex[:, 1]
        messages = transformed[src] + edgeMsg
        aggregated = jax.ops.segment_sum(messages, dst, num_segments=nodeFeatures.shape[0])
        return jax.nn.relu(aggregated)
    edge_index = jnp.stack([src, dst])
    edge_index_t = jnp.stack([src, dst], axis=1)
    h = jnp.maximum(_layernorm(x, axis=-1), 0.0)
    x = x + _L0_gnn_ref(h, src, dst, L0_gnn_Wq, L0_gnn_bq, L0_gnn_Wk, L0_gnn_bk, L0_gnn_Wv, L0_gnn_bv, L0_gnn_Ws, L0_gnn_bs, L0_gnn_Wg, L0_gnn_bg, L0_gnn_gamma, L0_gnn_beta, L0_gnn_alpha)
    h = jnp.maximum(_layernorm(x, axis=-1), 0.0)
    x = x + _L1_gnn_ref(h, L1_gnn_weight, L1_gnn_self_weight, edge_index, edge_type_8)
    h = jnp.maximum(_layernorm(x, axis=-1), 0.0)
    x = x + _L2_gnn_ref(h, edge_attr_16, L2_gnn_W_edge, L2_gnn_b_edge, L2_gnn_W1, L2_gnn_b1, L2_gnn_gamma, L2_gnn_beta, L2_gnn_W2, L2_gnn_b2, edge_index, 0, 4)
    h = jnp.maximum(_layernorm(x, axis=-1), 0.0)
    x = x + _L3_gnn_ref(h, edge_index_t, edge_attr_6, L3_gnn_W, L3_gnn_b, L3_gnn_We, L3_gnn_be)
    return x

_drawn_inputs = setup_inputs


def setup_inputs(seed=0):
    import zlib

    import numpy as np

    out = dict(_drawn_inputs(seed))
    spreads = {'L0_gnn_bq': (0.0, 2.0),
     'L0_gnn_bk': (0.0, 0.8),
     'L0_gnn_bv': (0.0, 0.1),
     'L0_gnn_bs': (0.0, 0.289),
     'L0_gnn_gamma': (1.0, 0.2),
     'L0_gnn_beta': (0.0, 0.273),
     'L2_gnn_b_edge': (0.0, 0.8),
     'L2_gnn_b1': (0.0, 2.0),
     'L2_gnn_gamma': (1.0, 0.56),
     'L2_gnn_beta': (0.0, 0.589),
     'L2_gnn_b2': (0.0, 0.305)}
    factors = {'L0_gnn_Wq': 3.491, 'L0_gnn_Wk': 3.47}
    for name, (base, spread) in spreads.items():
        noise = np.random.default_rng([zlib.crc32(name.encode()), seed]).standard_normal(out[name].shape)
        drawn = base * np.exp(spread * noise) if base else spread * noise
        out[name] = jnp.asarray(drawn.astype(out[name].dtype))
    for name, factor in factors.items():
        out[name] = (out[name] * factor).astype(out[name].dtype)
    return out
```

```python
from contextlib import ExitStack

import numpy as np

import concourse.bass as bass
from concourse import mybir
from concourse.alu_op_type import AluOpType as ALU

P = 128
F = 128
N = 12500
E = 200000
R = 8
H = 4
D = F // H
W = -(-N // P)
NP = W * P
ET = -(-E // P)
LAST = N - (W - 1) * P

GT = 4
BODY = 16
RING = 8
NREC = 4
RG = 4
TILES = -(-(ET * P + W * (P - 1)) // P)
GROUPS = -(-TILES // (GT * BODY)) * BODY
NT = GROUPS * GT
LEAD = 3
TP = NT + RG * GT
CH = 100

IDX, IDX8, LOC, TYP, ONE, ATT = range(6)
CD = ATT + 6
CS = ATT + 16

CREDIT = 32
NONE = -1.0e30
EPS = 1e-5

F32, BF16, I32, I16 = mybir.dt.float32, mybir.dt.bfloat16, mybir.dt.int32, mybir.dt.int16
ACT = mybir.ActivationFunctionType
AX = mybir.AxisListType.X


class Lane:

    def __init__(self, sem):
        self.sem, self.n, self.ops, self.seen = sem, 0, [], {}

    def wait(self, *tokens):
        for sem, value in tokens:
            if self.seen.get(id(sem), 0) < value:
                self.seen[id(sem)] = value
                self.ops.append(lambda e, s=sem, v=value: e.wait_ge(s, v))

    def do(self, what, *tokens):
        self.wait(*tokens)
        self.n += 1
        self.ops.append(lambda e, s=self.sem: what(e).then_inc(s, 1))
        return self.sem, self.n

    def dma(self, what, counter, *tokens):
        self.wait(*tokens)
        counter.n += 16
        self.ops.append(lambda e, s=counter.sem: what(e).then_inc(s, 16))
        return counter.sem, counter.n

    def play(self, engine):
        for op in self.ops:
            op(engine)
        self.ops = []


class Counter:
    def __init__(self, sem):
        self.sem, self.n = sem, 0

    @property
    def token(self):
        return self.sem, self.n


class Turn:

    def __init__(self, e, value, phase):
        self.e, self.value, self.times, self.phase = e, value, {}, phase
        self.sum = e.alloc_register(f"sum_{phase}")

    def multiple(self, per):
        if per not in self.times:
            self.times[per] = self.e.alloc_register(f"turn_{per}_{self.phase}")
            self.e.reg_mul(self.times[per], self.e.to_reg(self.value), per)
        return self.times[per]

    def close(self):
        for r in (self.sum, *self.times.values()):
            self.e.free_register(r)


class Group:

    def __init__(self, turn, j):
        self.turn, self.n, self.j = turn, j, j % BODY

    def count(self, sem, per, every, more):
        return sem, self.turn, BODY // every * per, self.n // every * per + more

    def tile(self, k):
        number = self.n * GT + k
        return self.turn.value * (BODY * GT) + number if self.turn else number


def until(e, mark):
    sem, turn, per, more = mark
    if turn is None:
        e.wait_ge(sem, more)
    else:
        e.reg_add(turn.sum, turn.multiple(per), more)
        e.wait_ge(sem, turn.sum)


def wide(ap, n):
    return ap.unsqueeze(2).to_broadcast([ap.shape[0], ap.shape[1], n])


def over(ap, m):
    return ap.unsqueeze(1).to_broadcast([ap.shape[0], m, ap.shape[1]])


class Core:
    pass


def build_program(nc, a, out, upto=99):
    ctx = ExitStack()
    with ctx:
        k = Core()
        k.nc, k.a, k.out = nc, a, out
        k.phase = 0
        k.sem = lambda name: ctx.enter_context(nc.semaphore(name))
        k.sb = scratch(k, ctx)
        k.dve, k.act, k.pe, k.pool, k.sp = (Lane(k.sem(f"s_{n}")) for n in ("dve", "act", "pe", "pool", "sp"))
        k.load = Counter(k.sem("s_load"))
        k.store = Counter(k.sem("s_store"))
        k.rec_dst = nc.dram_tensor("rec_dst", [P, TP, CD], F32).ap()
        k.rec_src = nc.dram_tensor("rec_src", [P, TP, CS], F32).ap()
        k.banks = ctx.enter_context(nc.psum_tensor("banks", [P, 8, 512], F32))
        k.psum = [k.banks[:, i, :] for i in range(8)]
        k.win_dst = k.sb("win_dst", [1, TP], I32)
        k.win_src = k.sb("win_src", [1, TP], I32)
        k.ring_sem = [k.sem(f"s_ring{i}") for i in range(RING)]
        k.ring_base = [0] * RING
        k.rec_sem = [k.sem(f"s_rec{i}") for i in range(NREC)]
        k.rec_base = [0] * NREC
        k.pass_sem, k.pass_base = {}, {}
        constants(k)
        sort_edges(k)
        if upto > 1:
            layers(k, upto)


def scratch(k, ctx):
    k.phase += 1
    return lambda name, shape, dt=F32: ctx.enter_context(k.nc.sbuf_tensor(f"{name}_{k.phase}", shape, dt))


def run_lanes(k):
    with k.nc.Block() as block:
        block.sync(lambda e: k.sp.play(e))
        block.gpsimd(lambda e: k.pool.play(e))
        block.scalar(lambda e: k.act.play(e))
        block.vector(lambda e: k.dve.play(e))
        block.tensor(lambda e: k.pe.play(e))


def constants(k):
    pool, dve = k.pool, k.dve
    k.col_i = k.sb("col_i", [P, P], I32)
    k.col = k.sb("col", [P, P])
    k.col_b = k.sb("col_b", [P, P], BF16)
    k.ident = k.sb("ident", [P, P])
    k.ident_b = k.sb("ident_b", [P, P], BF16)
    k.none4 = k.sb("none4", [P, H, P], BF16)
    k.ones = k.sb("ones", [P, P])
    k.before = k.sb("before", [P, P])
    t_col = pool.do(lambda e: e.iota(k.col_i[:, :], [[1, P]], base=0, channel_multiplier=0))
    t_one = pool.do(lambda e: e.memset(k.ones[:, :], 1.0))
    t_z = pool.do(lambda e: e.memset(k.ident[:, :], 0.0))
    t_id = pool.do(lambda e: e.affine_select(out=k.ident[:, :], in_=k.ident[:, :], compare_op=ALU.not_equal,
                                             fill=1.0, base=0, pattern=[[-1, P]], channel_multiplier=1), t_z)
    t_tri = pool.do(lambda e: e.affine_select(out=k.before[:, :], in_=k.ones[:, :], compare_op=ALU.is_ge,
                                              fill=0.0, base=-1, pattern=[[1, P]], channel_multiplier=-1), t_one)
    dve.do(lambda e: e.tensor_copy(k.col[:, :], k.col_i[:, :]), t_col)
    dve.do(lambda e: e.tensor_copy(k.col_b[:, :], k.col_i[:, :]), t_col)
    t_ib = dve.do(lambda e: e.tensor_copy(k.ident_b[:, :], k.ident[:, :]), t_id)
    dve.do(lambda e: e.tensor_scalar(k.none4[:, :, :], over(k.ident_b[:, :], H), NONE, None, ALU.mult), t_ib, t_tri)
    run_lanes(k)


def sort_edges(k):
    nc, dve, act, pe, pool, sp = k.nc, k.dve, k.act, k.pe, k.pool, k.sp
    with ExitStack() as ctx:
        sb = scratch(k, ctx)
        typ_i = sb("typ_i", [P, ET], I32)
        typ = sb("typ", [P, ET])
        node_i = {s: sb(f"node_{s}", [P, ET], I32) for s in ("src", "dst")}
        idx8 = {s: sb(f"idx8_{s}", [P, ET], I32) for s in ("src", "dst")}
        loc = {s: sb(f"loc_{s}", [P, ET]) for s in ("src", "dst")}
        row = {s: sb(f"row_{s}", [P, ET], I32) for s in ("src", "dst")}
        tmp_i = sb("tmp_i", [P, ET], I32)
        win = sb("win", [P, ET], BF16)
        hit = sb("hit", [P, 2, ET], BF16)
        rank = sb("rank", [P, 2, ET])
        slot = sb("slot", [P, ET])
        count = sb("count", [P, W])
        total = sb("total", [P, W])
        tiles_i = sb("tiles_i", [P, W], I32)
        tiles = sb("tiles", [P, W])
        ends = sb("ends", [P, W])
        base = sb("base", [P, W])
        end_col = sb("end_col", [W, 1])
        step_i = sb("step_i", [W, TP], I32)
        passed = sb("passed", [W, TP])
        blank = {"dst": sb("blank_d", [P, RG * GT, CD]), "src": sb("blank_s", [P, RG * GT, CS])}
        att = sb("att", [P, 2, CH, 16])
        stage = {"dst": sb("stage_d", [P, 2, CH, CD]), "src": sb("stage_s", [P, 2, CH, CS])}
        rec = {"dst": k.rec_dst, "src": k.rec_src}
        width = {"dst": CD, "src": CS}
        windows = {"dst": k.win_dst, "src": k.win_src}
        s_att = [Counter(k.sem(f"s_att{i}")) for i in range(2)]
        s_sc = [Counter(k.sem(f"s_sc{i}")) for i in range(2)]
        s_fill = {s: Counter(k.sem(f"s_fill_{s}")) for s in ("src", "dst")}

        for name, to in (("src", node_i["src"]), ("dst", node_i["dst"]), ("edge_type_8", typ_i)):
            t_in = sp.dma(lambda e, n=name, to=to: e.dma_start(to[:, :], k.a[n].rearrange("(p t) -> p t", p=P)), k.load)

        t_fill = {}
        for s in ("src", "dst"):
            t = pool.do(lambda e, s=s: e.memset(blank[s][:, :, :], 0.0))
            t = pool.do(lambda e, s=s: e.memset(blank[s][:, :, LOC:LOC + 1], -1.0), t)
            for b in range(0, TP, RG * GT):
                t_fill[s] = sp.dma(lambda e, s=s, b=b: e.dma_start(rec[s][:, b:b + RG * GT, :], blank[s][:, :, :]), s_fill[s], t)
        t_step = pool.do(lambda e: e.iota(step_i[:, :], [[1, TP]], base=0, channel_multiplier=0))
        t_st = {}
        for s in ("src", "dst"):
            t_st[s] = pool.do(lambda e, s=s: e.memset(stage[s][:, :, :, :], 1.0))

        t_typ = dve.do(lambda e: e.tensor_copy(typ[:, :], typ_i[:, :]), t_in)
        t_row, t_ready = {}, {}
        t_prev = None
        for s in ("src", "dst"):
            far = "dst" if s == "src" else "src"
            t = dve.do(lambda e, s=s: e.tensor_scalar(tmp_i[:, :], node_i[s][:, :], 7, None, ALU.arith_shift_right), *([t_prev] if t_prev else []))
            t = dve.do(lambda e: e.tensor_copy(win[:, :], tmp_i[:, :]), t)
            t = dve.do(lambda e, s=s: e.tensor_scalar(tmp_i[:, :], node_i[s][:, :], P - 1, None, ALU.bitwise_and), t)
            dve.do(lambda e, s=s: e.tensor_copy(loc[s][:, :], tmp_i[:, :]), t)
            t = dve.do(lambda e, s=s, f=far: e.scalar_tensor_tensor(out=idx8[s][:, :], in0=node_i[f][:, :], scalar=float(R),
                                                                    in1=typ_i[:, :], op0=ALU.mult, op1=ALU.add))
            for w in range(W):
                t = dve.do(lambda e, w=w: e.tensor_scalar(hit[:, w % 2, :], win[:, :], float(w), 0.0, ALU.is_equal, ALU.add,
                                                          accum_out=count[:, w:w + 1]), *([t] if w < 2 else [t_b[w % 2]]))
                t_b = [t, t] if w == 0 else [t if w % 2 == i else t_b[i] for i in range(2)]
            pt, pb = k.psum[0], k.psum[1]
            t_t = pe.do(lambda e: e.matmul(pt[:, 0:W], k.ones[:, :], count[:, :], start=True, stop=True), t, (dve.sem, dve.n))
            t_p = pe.do(lambda e: e.matmul(pb[:, 0:W], k.before[:, :], count[:, :], start=True, stop=True))
            t = dve.do(lambda e: e.tensor_scalar(total[:, :], pt[:, 0:W], float(P - 1), None, ALU.add), t_t)
            t = dve.do(lambda e: e.tensor_copy(tiles_i[:, :], total[:, :]), t)
            t = dve.do(lambda e: e.tensor_scalar(tiles_i[:, :], tiles_i[:, :], 7, None, ALU.arith_shift_right), t)
            t = dve.do(lambda e: e.tensor_copy(tiles[:, :], tiles_i[:, :]), t)
            t_e = dve.do(lambda e: e.tensor_tensor_scan(ends[:, :], tiles[:, :], tiles[:, :], 0.0, ALU.add, ALU.bypass), t)
            t = dve.do(lambda e: e.tensor_tensor(base[:, :], ends[:, :], tiles[:, :], ALU.subtract), t_e)
            t = dve.do(lambda e: e.tensor_scalar(base[:, :], base[:, :], float(P), -1.0, ALU.mult, ALU.add), t)
            t = dve.do(lambda e: e.tensor_tensor(base[:, :], base[:, :], pb[:, 0:W], ALU.add), t, t_p)
            t_sl = None
            t_h, t_k, t_s = [t, t], [t, t], [t, t]
            for w in range(W):
                b = w % 2
                t_h[b] = dve.do(lambda e, w=w, b=b: e.tensor_scalar(hit[:, b, :], win[:, :], float(w), None, ALU.is_equal), t_s[b])
                t_k[b] = dve.do(lambda e, w=w, b=b: e.tensor_tensor_scan(rank[:, b, :], hit[:, b, :], hit[:, b, :], base[:, w:w + 1],
                                                                         ALU.add, ALU.bypass), t_h[b])
                t_s[b] = dve.do(lambda e, w=w, b=b: e.copy_predicated(slot[:, :], hit[:, b, :].bitcast(I16), rank[:, b, :]),
                                t_k[b], t_s[1 - b])
            t = dve.do(lambda e, s=s: e.tensor_copy(row[s][:, :], slot[:, :]), t_s[0], t_s[1])
            t = dve.do(lambda e, s=s: e.tensor_scalar(tmp_i[:, :], row[s][:, :], 7, None, ALU.arith_shift_right), t)
            t = dve.do(lambda e, s=s: e.tensor_scalar(row[s][:, :], row[s][:, :], P - 1, None, ALU.bitwise_and), t)
            t_row[s] = t_prev = dve.do(lambda e, s=s: e.scalar_tensor_tensor(out=row[s][:, :], in0=row[s][:, :], scalar=float(TP),
                                                                    in1=tmp_i[:, :], op0=ALU.mult, op1=ALU.add), t)
            t_tr = pe.do(lambda e: e.transpose(pt[0:W, 0:P], ends[:, :], k.ident[:, :]), t_e, t_t)
            t = dve.do(lambda e: e.tensor_copy(end_col[:, :], pt[0:W, 0:1]), t_tr)
            t = dve.do(lambda e: e.tensor_scalar(passed[:, :], step_i[:, :], end_col[:, 0:1], None, ALU.is_ge), t, t_step)
            for c in range(0, TP, 512):
                n = min(512, TP - c)
                t_w = pe.do(lambda e, c=c, n=n: e.matmul(k.psum[2][0:1, 0:n], k.ones[0:W, 0:1], passed[:, c:c + n], start=True, stop=True), t, t_prev)
                t_prev = dve.do(lambda e, c=c, n=n, s=s: e.tensor_copy(windows[s][:, c:c + n], k.psum[2][0:1, 0:n]), t_w)
                t = t_prev

        j = 0
        t_stage = [(pool.sem, pool.n)] * 2
        t_sc = [None, None]
        t_cp = [None, None]
        for s in ("src", "dst"):
            far = "dst" if s == "src" else "src"
            na = width[s] - ATT
            attr = k.a["edge_attr_16" if s == "src" else "edge_attr_6"].rearrange("(p t) c -> p t c", p=P)
            flat = rec[s].rearrange("p t c -> (p t) c")
            for c in range(0, ET, CH):
                n, b = min(CH, ET - c), j % 2
                j += 1
                t_a = sp.dma(lambda e, b=b, c=c, n=n, na=na, attr=attr: e.dma_start(
                    att[:, b, :, :].rearrange("p t c -> p (t c)")[:, 0:n * na].rearrange("p (t c) -> p t c", c=na),
                    attr[:, c:c + n, :]), s_att[b], *([t_cp[b]] if t_cp[b] else []))
                wait = [t_st[s], t_row[s]] + ([t_sc[b]] if t_sc[b] else [])
                act.do(lambda e, s=s, b=b, c=c, n=n, f=far: e.copy(stage[s][:, b, 0:n, IDX].bitcast(I32), node_i[f][:, c:c + n]), *wait)
                act.do(lambda e, s=s, b=b, c=c, n=n: e.copy(stage[s][:, b, 0:n, IDX8].bitcast(I32), idx8[s][:, c:c + n]))
                act.do(lambda e, s=s, b=b, c=c, n=n: e.copy(stage[s][:, b, 0:n, LOC], loc[s][:, c:c + n]))
                act.do(lambda e, s=s, b=b, c=c, n=n: e.copy(stage[s][:, b, 0:n, TYP], typ[:, c:c + n]), t_typ)
                t_cp[b] = act.do(lambda e, s=s, b=b, n=n, na=na: e.copy(
                    stage[s][:, b, 0:n, ATT:ATT + na],
                    att[:, b, :, :].rearrange("p t c -> p (t c)")[:, 0:n * na].rearrange("p (t c) -> p t c", c=na)), t_a)
                for i in range(n):
                    t_sc[b] = pool.dma(lambda e, s=s, b=b, i=i, c=c, flat=flat: e.indirect_dma_start(
                        out=flat, out_offset=bass.IndirectOffsetOnAxis(ap=row[s][:, c + i:c + i + 1], axis=0),
                        in_=stage[s][:, b, i, :], in_offset=None), s_sc[b], t_cp[b], t_fill[s])
        pool.wait(t_sc[0], t_sc[1])
        run_lanes(k)



class Pass:

    def __init__(self, k, rec, cols, win, row, leads):
        self.k, self.rec, self.cols, self.win, self.row, self.leads = k, rec, cols, win, row, leads
        self.stages = {e: [] for e in ("vector", "scalar", "tensor")}
        self.per = {}
        self.credit = []
        self.leads_of = {}

    def at(self, name, group, nth=None):
        per = self.per[name]
        more = (per if nth is None else nth) + self.k.pass_base.get(name, 0)
        return group.count(self.k.pass_sem[name], per, 1, more)

    def at_before(self, name, group, depth, nth=None):
        sem, turn, per, more = self.at(name, group, nth)
        more -= depth * self.per[name]
        if turn is None:
            more = max(more, self.k.pass_base[name])
        return sem, turn, per, more

    def record(self, group):
        b = group.j // RG % NREC
        return group.count(self.k.rec_sem[b], 16, RG * NREC, 16 + self.k.rec_base[b])

    def gathered(self, group):
        b = group.j % RING
        return group.count(self.k.ring_sem[b], 16 * GT, RING, 16 * GT + self.k.ring_base[b])

    def rows(self, group, lo, hi):
        b = group.j // RG % NREC
        t = group.j % RG * GT
        return self.recs[:, b, t:t + GT, lo:hi]

    def stage(self, engine, name, per, lead, work):
        self.per[name] = per
        self.k.pass_sem.setdefault(name, None)
        if self.k.pass_sem[name] is None:
            self.k.pass_sem[name] = self.k.sem(f"p_{name}")
            self.k.pass_base[name] = CREDIT
            self.credit.append((engine, name))
        self.stages[engine].append((lead, name, work))
        self.leads_of[name] = lead

    def run(self, table, gather_lead, freed, last):
        k = self.k
        blocks = GROUPS // RG + 1
        gathers = GROUPS + gather_lead if table is not None else 0

        def play(engine, e):
            for owner, name in self.credit:
                if owner == engine:
                    e.sem_inc(k.pass_sem[name], CREDIT)
            for step in range(-self.leads, 0):
                for lead, _, work in self.stages[engine]:
                    if step + lead >= 0:
                        work(e, Group(None, step + lead))
            with e.Fori(0, GROUPS // BODY) as value:
                turn = Turn(e, value, k.phase)
                for j in range(BODY):
                    for lead, _, work in self.stages[engine]:
                        work(e, Group(turn, j + lead))
                turn.close()

        def sync(e):
            for c in range(blocks):
                if c >= NREC:
                    until(e, self.at(last, Group(None, (c - NREC) * RG + RG - 1)))
                e.dma_start(self.recs[:, c % NREC, :, :],
                            self.rec[:, c * RG * GT:(c + 1) * RG * GT, :]).then_inc(k.rec_sem[c % NREC], 16)
            for b in range(NREC):
                n = len(range(b, blocks, NREC))
                k.rec_base[b] += 16 * n
                e.wait_ge(k.rec_sem[b], k.rec_base[b])

        def gpsimd(e):
            for g in range(gathers):
                group = Group(None, g)
                if g % RG == 0:
                    until(e, self.record(group))
                if g >= RING:
                    until(e, self.at(freed, Group(None, g - RING)))
                for t in range(GT):
                    index = self.rows(group, self.row, self.row + 1)[:, t, :].bitcast(I32)
                    e.indirect_dma_start(out=self.far[:, g % RING, t, :], out_offset=None, in_=table,
                                         in_offset=bass.IndirectOffsetOnAxis(ap=index, axis=0)
                                         ).then_inc(k.ring_sem[g % RING], 16)
            for b in range(RING):
                if gathers:
                    e.wait_ge(k.ring_sem[b], k.ring_base[b] + 16 * GT * len(range(b, gathers, RING)))

        with k.nc.Block() as block:
            block.gpsimd(gpsimd)
            block.vector(lambda e: play("vector", e))
            block.scalar(lambda e: play("scalar", e))
            block.tensor(lambda e: play("tensor", e))
            block.sync(sync)
        for b in range(RING):
            k.ring_base[b] += 16 * GT * len(range(b, gathers, RING))
        for name, lead in self.leads_of.items():
            k.pass_base[name] += (GROUPS + lead) * self.per[name]


def count_pass(k, rec, cols, win, counts):
    with ExitStack() as ctx:
        sb = scratch(k, ctx)
        ps = Pass(k, rec, cols, win, IDX, LEAD)
        ps.recs = sb("recs", [P, NREC, RG * GT, cols])
        hot = sb("hot", [P, RING, GT, P], BF16)
        kind = sb("kind", [P, RING, GT, R], BF16)

        def mark(e, g):
            until(e, ps.record(g))
            b = g.j % RING
            e.tensor_tensor(kind[:, b, :, :], over(k.col[:, 0:R], GT), ps.rows(g, TYP, TYP + 1).to_broadcast([P, GT, R]), ALU.is_equal)
            e.tensor_tensor(hot[:, b, :, :], over(k.col[:, :], GT), ps.rows(g, LOC, LOC + 1).to_broadcast([P, GT, P]), ALU.is_equal
                            ).then_inc(k.pass_sem["mark"], 1)

        def product(e, g):
            until(e, ps.at("mark", g))
            until(e, ps.at_before("sum", g, 4))
            bank = k.psum[g.j % 4]
            for t in range(GT):
                m = e.matmul(bank[:, t * R:(t + 1) * R], hot[:, g.j % RING, t, :], kind[:, g.j % RING, t, :], start=True, stop=True)
            m.then_inc(k.pass_sem["product"], 1)

        def gather_up(e, g):
            at = windows_of(e, win, g)
            until(e, ps.at("product", g))
            for t in range(GT):
                w = at[t]
                until(e, ps.at("sum", g, t))
                e.tensor_tensor(counts[:, bass.ds(w, 1), :], k.psum[g.j % 4][:, t * R:(t + 1) * R].unsqueeze(1),
                                counts[:, bass.ds(w, 1), :], ALU.add).then_inc(k.pass_sem["sum"], 1)

        ps.stage("vector", "mark", 1, 3, mark)
        ps.stage("tensor", "product", 1, 1, product)
        ps.stage("vector", "sum", GT, 0, gather_up)
        ps.run(None, 0, None, "sum")


def windows_of(e, win, g):
    return e.bass.values_load_multi_w_load_instructions(win[0:1, bass.ds(g.tile(0), GT)], engines=[e.engine],
                                                        min_val=0, max_val=W)[1]


def sum_pass(k, rec, cols, win, table, acc, extra):
    n_all = F + extra
    with ExitStack() as ctx:
        sb = scratch(k, ctx)
        ps = Pass(k, rec, cols, win, IDX, LEAD)
        ps.recs = sb("recs", [P, NREC, RG * GT, cols])
        ps.far = sb("far", [P, RING, GT, F])
        hot = sb("hot", [P, RING, GT, P])

        def bank(g, t):
            at = t % 2 * n_all
            return k.psum[g.j % 4 * 2 + t // 2][:, at:at + n_all]

        def mark(e, g):
            until(e, ps.record(g))
            e.tensor_tensor(hot[:, g.j % RING, :, :], over(k.col[:, :], GT), ps.rows(g, LOC, LOC + 1).to_broadcast([P, GT, P]),
                            ALU.is_equal).then_inc(k.pass_sem["mark"], 1)

        def product(e, g):
            until(e, ps.at("mark", g))
            until(e, ps.gathered(g))
            until(e, ps.at_before("sum", g, 4))
            b = g.j % RING
            for t in range(GT):
                e.matmul(bank(g, t)[:, 0:F], hot[:, b, t, :], ps.far[:, b, t, :], start=True, stop=True)
                m = e.matmul(bank(g, t)[:, F:n_all], hot[:, b, t, :], ps.rows(g, ONE, ONE + extra)[:, t, :], start=True, stop=True)
            m.then_inc(k.pass_sem["product"], 1)

        def gather_up(e, g):
            at = windows_of(e, win, g)
            until(e, ps.at("product", g))
            for t in range(GT):
                w = at[t]
                until(e, ps.at("sum", g, t))
                e.tensor_tensor(acc[:, bass.ds(w, 1), :], bank(g, t).unsqueeze(1), acc[:, bass.ds(w, 1), :],
                                ALU.add).then_inc(k.pass_sem["sum"], 1)

        ps.stage("vector", "mark", 1, 3, mark)
        ps.stage("tensor", "product", 1, 1, product)
        ps.stage("vector", "sum", GT, 0, gather_up)
        ps.run(table, 1, "product", "sum")


def relation_pass(k, rec, cols, win, table, acc):
    with ExitStack() as ctx:
        sb = scratch(k, ctx)
        ps = Pass(k, rec, cols, win, IDX8, LEAD)
        ps.recs = sb("recs", [P, NREC, RG * GT, cols])
        ps.far = sb("far", [P, RING, GT, F])
        hot = sb("hot", [P, 4, GT, P], BF16)
        kind = sb("kind", [P, 4, GT, R])
        hot_t = sb("hot_t", [P, 4, GT, P])
        part = sb("part", [P, 2, GT, R])
        share = sb("share", [P, 2, GT])
        hot_s = sb("hot_s", [P, 4, GT, P])
        turned = [k.psum[i][:, 0:256].bitcast(BF16).rearrange("p (t n) -> p t n", t=GT) for i in (0, 1)]
        shares = [k.psum[i][:, 0:GT * R].rearrange("p (t r) -> p t r", t=GT) for i in (2, 3)]
        sums = [k.psum[i][:, :].rearrange("p (t f) -> p t f", t=GT) for i in (4, 5, 6, 7)]

        def mark(e, g):
            until(e, ps.record(g))
            b = g.j % 4
            e.tensor_tensor(kind[:, b, :, :], over(k.col[:, 0:R], GT), ps.rows(g, TYP, TYP + 1).to_broadcast([P, GT, R]), ALU.is_equal)
            e.tensor_tensor(hot[:, b, :, :], over(k.col[:, :], GT), ps.rows(g, LOC, LOC + 1).to_broadcast([P, GT, P]), ALU.is_equal
                            ).then_inc(k.pass_sem["mark"], 1)

        def turn(e, g):
            until(e, ps.at("mark", g))
            until(e, ps.at_before("flat", g, 2))
            for t in range(GT):
                m = e.transpose(turned[g.j % 2][:, t, :], hot[:, g.j % 4, t, :], k.ident_b[:, :])
            m.then_inc(k.pass_sem["turn"], 1)

        def flat(e, g):
            until(e, ps.at("turn", g))
            e.copy(hot_t[:, g.j % 4, :, :], turned[g.j % 2]).then_inc(k.pass_sem["flat"], 1)

        def look_up(e, g):
            at = windows_of(e, win, g)
            until(e, ps.at("flat", g))
            until(e, ps.at_before("weigh", g, 2, 1))
            for t in range(GT):
                w = at[t]
                m = e.matmul(shares[g.j % 2][:, t, :], hot_t[:, g.j % 4, t, :], k.inverse[:, bass.ds(w, 1), :].rearrange("p a r -> p (a r)"),
                             start=True, stop=True)
            m.then_inc(k.pass_sem["look"], 1)

        def weigh(e, g):
            b, b4 = g.j % 2, g.j % 4
            until(e, ps.at("look", g))
            e.tensor_tensor(part[:, b, :, :], shares[b], kind[:, b4, :, :], ALU.mult).then_inc(k.pass_sem["weigh"], 1)
            until(e, ps.at("weigh", g, 1))
            e.tensor_reduce(share[:, b, :], part[:, b, :, :], AX, ALU.add).then_inc(k.pass_sem["weigh"], 1)
            until(e, ps.at("weigh", g, 2))
            e.tensor_tensor(hot_s[:, b4, :, :], hot[:, b4, :, :], wide(share[:, b, :], P), ALU.mult).then_inc(k.pass_sem["weigh"], 1)

        def product(e, g):
            until(e, ps.at("weigh", g))
            until(e, ps.gathered(g))
            until(e, ps.at_before("sum", g, 4))
            for t in range(GT):
                m = e.matmul(sums[g.j % 4][:, t, :], hot_s[:, g.j % 4, t, :], ps.far[:, g.j % RING, t, :], start=True, stop=True)
            m.then_inc(k.pass_sem["product"], 1)

        def gather_up(e, g):
            at = windows_of(e, win, g)
            until(e, ps.at("product", g))
            for t in range(GT):
                w = at[t]
                until(e, ps.at("sum", g, t))
                e.tensor_tensor(acc[:, bass.ds(w, 1), :], sums[g.j % 4][:, t:t + 1, :], acc[:, bass.ds(w, 1), :],
                                ALU.add).then_inc(k.pass_sem["sum"], 1)

        ps.stage("vector", "mark", 1, 3, mark)
        ps.stage("vector", "weigh", 3, 1, weigh)
        ps.stage("scalar", "flat", 1, 3, flat)
        ps.stage("tensor", "product", 1, 0, product)
        ps.stage("tensor", "look", 1, 2, look_up)
        ps.stage("tensor", "turn", 1, 3, turn)
        ps.stage("vector", "sum", GT, 0, gather_up)
        ps.run(table, 0, "product", "sum")


def attention_pass(k, rec, cols, win, table, keys, top, acc, counts):
    D1 = D + 1
    with ExitStack() as ctx:
        sb = scratch(k, ctx)
        ps = Pass(k, rec, cols, win, IDX, LEAD)
        ps.recs = sb("recs", [P, NREC, RG * GT, cols])
        ps.far = sb("far", [P, RING, GT, 2 * F])
        hot = sb("hot", [P, 4, GT, P], BF16)
        hot_f = sb("hot_f", [P, 4, GT, P])
        cold = sb("cold", [P, 2, GT, P], BF16)
        hot_t = sb("hot_t", [P, 4, GT, P])
        qk = sb("qk", [P, 1, GT, F])
        score = sb("score", [P, 4, GT * H])
        s_hi = sb("s_hi", [P, 2, GT * H], BF16)
        s_lo = sb("s_lo", [P, 2, GT * H], BF16)
        kind = sb("kind", [P, 4, GT, R], BF16)
        tile_top4 = sb("tile_top", [P, 2, GT, H])
        tile_top = tile_top4[:, :, :, :]
        old_top = sb("old_top", [P, 2, GT, H])
        tops_at = {}
        new_top = sb("new_top", [P, 2, GT, H])
        drop = sb("drop", [P, 2, GT, H])
        over_top = sb("over_top", [P, 2, GT * H])
        mix = sb("mix", [P, 2, GT * H, D1])
        sums = [[k.psum[i][:, t * H * D1:(t + 1) * H * D1].rearrange("p (h d) -> p h d", h=H) for t in (0, 1)] for i in (0, 1)]
        key_rows = k.psum[2][:, :].rearrange("p (t f) -> p t f", t=GT)
        turned = k.psum[3][:, 0:256].bitcast(BF16).rearrange("p (t n) -> p t n", t=GT)
        top_rows = k.psum[0][:, 2 * H * D1:2 * H * D1 + GT * H]
        counted = k.psum[1][:, 2 * H * D1:2 * H * D1 + GT * R]
        spread = k.banks[:, 4:4 + GT, :]

        def mark(e, g):
            until(e, ps.record(g))
            until(e, ps.at_before("flat", g, 2))
            e.tensor_tensor(kind[:, g.j % 4, :, :], over(k.col[:, 0:R], GT), ps.rows(g, TYP, TYP + 1).to_broadcast([P, GT, R]), ALU.is_equal)
            e.tensor_tensor(hot[:, g.j % 4, :, :], over(k.col[:, :], GT), ps.rows(g, LOC, LOC + 1).to_broadcast([P, GT, P]),
                            ALU.is_equal).then_inc(k.pass_sem["mark"], 1)

        def score_products(e, g):
            until(e, ps.at("key", g))
            until(e, ps.gathered(g))
            e.tensor_tensor(qk[:, 0, :, :], ps.far[:, g.j % RING, :, 0:F], key_rows, ALU.mult).then_inc(k.pass_sem["score"], 1)

        def score_sums(e, g):
            until(e, ps.at("score", g, 1))
            e.tensor_reduce(score[:, g.j % 4, :], qk[:, 0, :, :].rearrange("p t (h d) -> p (t h) d", h=H), AX, ALU.add
                            ).then_inc(k.pass_sem["score"], 1)

        def score_high(e, g):
            until(e, ps.at("score", g, 2))
            until(e, ps.at_before("spread", g, 2))
            e.tensor_copy(s_hi[:, g.j % 2, :], score[:, g.j % 4, :]).then_inc(k.pass_sem["score"], 1)

        def score_low(e, g):
            until(e, ps.at("score", g, 3))
            e.tensor_tensor(s_lo[:, g.j % 2, :], score[:, g.j % 4, :], s_hi[:, g.j % 2, :], ALU.subtract
                            ).then_inc(k.pass_sem["score"], 1)

        def tile_tops(e, g):
            until(e, ps.at("spread", g))
            e.tensor_reduce(tile_top[:, g.j % 2, :, :].rearrange("p t h -> p (t h)"), spread.rearrange("p t (h n) -> p (t h) n", h=H), AX, ALU.max
                            ).then_inc(k.pass_sem["reduce"], 1)

        def running_tops(first):
            def work(e, g):
                b, step = g.j % 2, k.pass_sem["top"]
                if first == 0:
                    tops_at[g.j] = windows_of(e, win, g)
                    until(e, ps.at("reduce", g))
                    until(e, ps.at_before("fade", g, 2))
                for t in (first, first + 1):
                    mine = top[:, bass.ds(tops_at[g.j][t], 1), :].rearrange("p a h -> p (a h)")
                    until(e, ps.at("top", g, t))
                    e.tensor_tensor(old_top[:, b, t, :], mine, mine, ALU.max)
                    e.tensor_tensor(mine, mine, tile_top[:, b, t, :], ALU.max).then_inc(step, 1)
            return work

        def new_tops(e, g):
            b = g.j % 2
            until(e, ps.at("top", g, GT))
            e.tensor_tensor(new_top[:, b, :, :], old_top[:, b, :, :], tile_top[:, b, :, :], ALU.max).then_inc(k.pass_sem["top"], 1)

        def drops(e, g):
            b = g.j % 2
            until(e, ps.at("top", g, GT + 1))
            e.tensor_tensor(drop[:, b, :, :], old_top[:, b, :, :], new_top[:, b, :, :], ALU.subtract).then_inc(k.pass_sem["top"], 1)

        def below(e, g):
            until(e, ps.at("top_row", g))
            until(e, ps.at("score", g))
            e.tensor_tensor(over_top[:, g.j % 2, :], score[:, g.j % 4, :], top_rows, ALU.subtract).then_inc(k.pass_sem["below"], 1)

        def mixes(e, g):
            b = g.j % 2
            until(e, ps.at("weight", g))
            weight = mix[:, b, :, D].rearrange("p (t h) -> p t h", t=GT).unsqueeze(3).to_broadcast([P, GT, H, D])
            e.tensor_tensor(mix[:, b, :, 0:D].rearrange("p (t h) d -> p t h d", t=GT),
                            ps.far[:, g.j % RING, :, F:2 * F].rearrange("p t (h d) -> p t h d", h=H), weight, ALU.mult
                            ).then_inc(k.pass_sem["mix"], 1)

        def gather_up(e, g):
            at = windows_of(e, win, g)
            b = g.j % 2
            until(e, ps.at("product", g))
            until(e, ps.at("fade", g))
            for t in range(GT):
                mine = acc[:, bass.ds(at[t], 1), :].rearrange("p a (h d) -> p (a h) d", h=H)
                seen = counts[:, bass.ds(at[t], 1), :].rearrange("p a r -> p (a r)")
                until(e, ps.at("sum", g, t))
                e.tensor_tensor(seen, counted[:, t * R:(t + 1) * R], seen, ALU.add)
                for h in range(H):
                    m = e.scalar_tensor_tensor(out=mine[:, h, :], in0=mine[:, h, :], scalar=drop[:, b, t, h:h + 1],
                                               in1=sums[t // 2][t % 2][:, h, :], op0=ALU.mult, op1=ALU.add)
                m.then_inc(k.pass_sem["sum"], 1)

        def weights(e, g):
            until(e, ps.at("below", g))
            until(e, ps.at_before("product", g, 2))
            e.activation(mix[:, g.j % 2, :, D], over_top[:, g.j % 2, :], ACT.Exp).then_inc(k.pass_sem["weight"], 1)

        def flat(e, g):
            b, b4 = g.j % 2, g.j % 4
            until(e, ps.at("turn", g))
            until(e, ps.at_before("top_row", g, 4))
            e.copy(hot_t[:, b4, :, :], turned)
            until(e, ps.at_before("product", g, 4))
            e.copy(hot_f[:, b4, :, :], hot[:, b4, :, :])
            until(e, ps.at_before("spread", g, 2))
            e.activation(cold[:, b, :, :], hot[:, b4, :, :], ACT.Copy, bias=1.0, scale=-1.0).then_inc(k.pass_sem["flat"], 1)

        def fade(e, g):
            until(e, ps.at("top", g))
            until(e, ps.at_before("sum", g, 2))
            e.activation(drop[:, g.j % 2, :, :], drop[:, g.j % 2, :, :], ACT.Exp).then_inc(k.pass_sem["fade"], 1)

        def keys_of(e, g):
            at = windows_of(e, win, g)
            until(e, ps.at("flat", g))
            until(e, ps.at_before("score", g, 1))
            for t in range(GT):
                w = at[t]
                m = e.matmul(key_rows[:, t, :], hot_t[:, g.j % 4, t, :], keys[:, bass.ds(w, 1), :].rearrange("p a f -> p (a f)"),
                             start=True, stop=True)
            m.then_inc(k.pass_sem["key"], 1)

        def turn(e, g):
            until(e, ps.at("mark", g))
            until(e, ps.at_before("flat", g, 1))
            for t in range(GT):
                m = e.transpose(turned[:, t, :], hot[:, g.j % 4, t, :], k.ident_b[:, :])
            m.then_inc(k.pass_sem["turn"], 1)

        def top_row(e, g):
            until(e, ps.at("top", g, GT + 1))
            until(e, ps.at_before("below", g, 1))
            for t in range(GT):
                m = e.matmul(top_rows[:, t * H:(t + 1) * H], hot_t[:, g.j % 4, t, :], new_top[:, g.j % 2, t, :], start=True, stop=True)
            m.then_inc(k.pass_sem["top_row"], 1)

        def product(e, g):
            until(e, ps.at("mix", g))
            until(e, ps.at_before("sum", g, 1))
            for t in range(GT):
                e.matmul(counted[:, t * R:(t + 1) * R], hot[:, g.j % 4, t, :], kind[:, g.j % 4, t, :], start=True, stop=True)
                m = e.matmul(sums[t // 2][t % 2].rearrange("p h d -> p (h d)"), hot_f[:, g.j % 4, t, :],
                             mix[:, g.j % 2, t * H:(t + 1) * H, :].rearrange("p h d -> p (h d)"), start=True, stop=True)
            m.then_inc(k.pass_sem["product"], 1)

        def spreads(e, g):
            b = g.j % 2
            until(e, ps.at("score", g))
            until(e, ps.at_before("reduce", g, 1))
            for t in range(GT):
                e.matmul(spread[:, t, :], cold[:, b, t, :], k.none4[:, :, :].rearrange("p h n -> p (h n)"),
                         start=True, stop=False, skip_group_check=True)
                for h in range(H):
                    c = t * H + h
                    for s in (s_hi, s_lo):
                        m = e.matmul(spread[:, t, h * P:(h + 1) * P], s[:, b, c:c + 1].to_broadcast([P, P]), k.ident_b[:, :],
                                     start=False, stop=(h == H - 1 and s is s_lo), skip_group_check=True)
            m.then_inc(k.pass_sem["spread"], 1)

        ps.stage("vector", "mark", 1, 3, mark)
        ps.stage("vector", "below", 1, 0, below)
        ps.stage("vector", "score", 4, 2, score_products)
        ps.stage("vector", "reduce", 1, 1, tile_tops)
        ps.stage("vector", "score", 4, 2, score_sums)
        ps.stage("vector", "top", GT + 2, 1, running_tops(0))
        ps.stage("vector", "score", 4, 2, score_high)
        ps.stage("vector", "top", GT + 2, 1, running_tops(2))
        ps.stage("vector", "score", 4, 2, score_low)
        ps.stage("vector", "top", GT + 2, 1, new_tops)
        ps.stage("vector", "mix", 1, 0, mixes)
        ps.stage("vector", "top", GT + 2, 1, drops)
        ps.stage("vector", "sum", GT, 0, gather_up)
        ps.stage("scalar", "weight", 1, 0, weights)
        ps.stage("scalar", "flat", 1, 3, flat)
        ps.stage("scalar", "fade", 1, 1, fade)
        ps.stage("tensor", "key", 1, 2, keys_of)
        ps.stage("tensor", "turn", 1, 3, turn)
        ps.stage("tensor", "top_row", 1, 1, top_row)
        ps.stage("tensor", "product", 1, 0, product)
        ps.stage("tensor", "spread", 1, 2, spreads)
        ps.run(table, 2, "mix", "sum")



def root(k, variance, ready):
    t = k.dve.do(lambda e: e.tensor_scalar(variance, variance, EPS, None, ALU.add), ready)
    t = k.act.do(lambda e: e.activation(variance, variance, ACT.Sqrt), t)
    return k.dve.do(lambda e: e.reciprocal(variance, variance), t)


def normalize(k, x, stats, moments, n, ready):
    dve = k.dve
    for i in range(n):
        t = dve.do(lambda e, i=i: e.bn_stats(stats[:, i, :], x[:, i, :]), *ready)
    for i in range(n):
        t = dve.do(lambda e, i=i: e.bn_aggr(moments[:, i, :], stats[:, i, :]), t)
    t = root(k, moments[:, 0:n, 1], t)
    return dve.do(lambda e: e.scalar_tensor_tensor(out=moments[:, 0:n, 0], in0=moments[:, 0:n, 0], scalar=-1.0,
                                                   in1=moments[:, 0:n, 1], op0=ALU.mult, op1=ALU.mult), t)


def load_rows(k, pairs):
    for to, of in pairs:
        t = k.sp.dma(lambda e, to=to, of=of: e.dma_start(to, of), k.load)
    return t


def turn_window(k, source, bank, to, ready, bank_free, to_free):
    t = k.pe.do(lambda e: e.transpose(bank[:, 0:P], source, k.ident[:, :]), *ready, *bank_free)
    return k.act.do(lambda e: e.copy(to, bank[:, 0:P]), t, *to_free)


C7 = 7
assert W % C7 == 0


def attention_tables(k):
    dve, act, pe, sp, a = k.dve, k.act, k.pe, k.sp, k.a
    with ExitStack() as ctx:
        sb = scratch(k, ctx)
        w4 = sb("w4", [P, 4, F])
        b4 = sb("b4", [1, 4, F])
        xin = sb("xin", [P, 2, C7, F])
        stats = sb("stats", [P, 2, C7, 6])
        moments = sb("moments", [P, 2, C7, 2])
        h = sb("h", [P, 2, F])
        ht = sb("ht", [P, 2, F])
        qv = sb("qv", [P, 4, 2 * F])
        skip = sb("skip", [P, 4, F])
        names = ("q", "v", "k", "s")
        t_w = load_rows(k, [(w4[:, i, :], a[f"L0_gnn_W{c}"]) for i, c in enumerate(names)]
                        + [(b4[:, i, :], a[f"L0_gnn_b{c}"].rearrange("(a f) -> a f", a=1)) for i, c in enumerate(names)])
        x_rows = a["x"].rearrange("(w p) f -> p w f", p=P)
        qv_rows = k.table_qv.rearrange("(w p) f -> w p f", p=P)
        t_z = k.pool.do(lambda e: e.memset(k.keys[:, W, :], 0.0))
        t_x, t_h, t_ht, t_pe = [None] * (W // C7), {}, {}, {}
        t_norm, t_q, t_v = {}, {}, {}
        got = lambda d, i: [d[i]] if i in d else []

        def fetch(c):
            t_x[c] = sp.dma(lambda e: e.dma_start(xin[:, c % 2, :, :], x_rows[:, c * C7:(c + 1) * C7, :]),
                            k.x_in[c % 2], *got(t_h, (c - 1) * C7 - 1))
        fetch(0)
        for c in range(W // C7):
            if c + 1 < W // C7:
                fetch(c + 1)
            t_norm[c] = normalize(k, xin[:, c % 2, :, :], stats[:, c % 2, :, :], moments[:, c % 2, :, :], C7,
                                  [t_x[c], *got(t_h, (c - 1) * C7 - 1)])
            for i in range(C7):
                w = c * C7 + i
                b, s = w % 2, w % 4
                t_h[w] = act.do(lambda e, c=c, i=i, b=b: e.activation(
                    h[:, b, :], xin[:, c % 2, i, :], ACT.Relu, bias=moments[:, c % 2, i, 0:1], scale=moments[:, c % 2, i, 1:2]),
                    t_norm[c], *got(t_ht, w - 2))
                t_ht[w] = turn_window(k, h[:, b, :], k.psum[b], ht[:, b, :], [t_h[w]], got(t_ht, w - 2), got(t_pe, w - 2))
                bank = k.psum[2 + s]
                pe.do(lambda e, b=b, bank=bank: e.matmul(bank[:, :], ht[:, b, :], w4[:, :, :].rearrange("p a f -> p (a f)"), start=True, stop=False),
                      t_ht[w], t_w, *got(t_q, w - 4), *got(t_v, w - 4))
                t_pe[w] = pe.do(lambda e, bank=bank: e.matmul(bank[:, :], k.ones[0:1, :], b4[:, :, :].rearrange("p a f -> p (a f)"), start=False, stop=True))
                t_v[w] = dve.do(lambda e, s=s, bank=bank: e.tensor_copy(qv[:, s, :], bank[:, 0:2 * F]), t_pe[w], *got(k.t_qv, w - 4))
                act.do(lambda e, w=w, bank=bank: e.activation(k.keys[:, w, :], bank[:, 2 * F:3 * F], ACT.Copy, scale=float(D) ** -0.5), t_v[w])
                t_q[w] = act.do(lambda e, s=s, bank=bank: e.copy(skip[:, s, :], bank[:, 3 * F:4 * F]), *got(k.t_skip, w - 4))
                k.t_qv[w] = sp.dma(lambda e, w=w, s=s: e.dma_start(qv_rows[w], qv[:, s, :]), k.qv_out[s], t_v[w])
                k.t_skip[w] = sp.dma(lambda e, w=w, s=s: e.dma_start(k.skip[:, w, :], skip[:, s, :]), k.skip_out[s], t_q[w])
        for s in range(4):
            sp.wait(k.qv_out[s].token, k.skip_out[s].token)
        run_lanes(k)


def attention_end(k):
    dve, act, sp, a = k.dve, k.act, k.sp, k.a
    with ExitStack() as ctx:
        sb = scratch(k, ctx)
        wg = sb("wg", [P, 3, F])
        w_skip, w_agg = sb("w_skip", [P, F]), sb("w_agg", [P, F])
        bg, alpha = sb("bg", [P, 1]), sb("alpha", [P, 1])
        gamma, beta = sb("gamma", [P, F]), sb("beta", [P, F])
        skip = sb("skip", [P, 2, C7, F])
        agg = sb("agg", [P, C7, F])
        tmp = sb("tmp", [P, C7, F])
        tmp2 = sb("tmp2", [P, C7, F])
        den = sb("den", [P, C7 * H])
        z = sb("z", [P, 2, C7])
        stats = sb("stats", [P, C7, 6])
        moments = sb("moments", [P, C7, 2])
        every = lambda name, n: a[name].rearrange("(a n) -> a n", a=1).to_broadcast([P, n])
        x_rows = a["x"].rearrange("(w p) f -> p w f", p=P)
        load_rows(k, [(k.x[:, 0:W, :], x_rows),
                      (wg[:, :, :].rearrange("p a f -> p (a f)"), a["L0_gnn_Wg"].rearrange("n a -> a n").to_broadcast([P, 3 * F])),
                      (bg[:, :], every("L0_gnn_bg", 1)), (alpha[:, :], every("L0_gnn_alpha", 1)),
                      (gamma[:, :], every("L0_gnn_gamma", F))])
        t_w = load_rows(k, [(beta[:, :], every("L0_gnn_beta", F))])
        dve.do(lambda e: e.tensor_tensor(w_skip[:, :], wg[:, 0, :], wg[:, 2, :], ALU.add), t_w)
        t = dve.do(lambda e: e.tensor_tensor(w_agg[:, :], wg[:, 1, :], wg[:, 2, :], ALU.subtract))
        sums = k.acc_flat[:, 0:W * H * (D + 1)].rearrange("p (g d) -> p g d", d=D + 1)
        flat = lambda ap: ap.rearrange("p w (h d) -> p (w h) d", h=H)
        t_s, t_use = {}, {}

        def fetch(c):
            t_s[c] = sp.dma(lambda e: e.dma_start(skip[:, c % 2, :, :], k.skip[:, c * C7:(c + 1) * C7, :]), k.x_in[c % 2],
                            *([t_use[c - 2]] if c >= 2 else []))
        fetch(0)
        fetch(1)
        for c in range(W // C7):
            g = c * C7 * H
            b = c % 2
            s = skip[:, b, :, :]
            mine = sums[:, g:g + C7 * H, :]
            x = k.x[:, c * C7:(c + 1) * C7, :]
            t = dve.do(lambda e, m=mine: e.tensor_scalar(den[:, :], m[:, :, D], 0.0, None, ALU.is_equal), t)
            t = dve.do(lambda e, m=mine: e.tensor_tensor(den[:, :], den[:, :], m[:, :, D], ALU.add), t)
            t = dve.do(lambda e: e.reciprocal(den[:, :], den[:, :]), t)
            t = dve.do(lambda e, m=mine: e.tensor_tensor(flat(agg[:, :, :]), m[:, :, 0:D], wide(den[:, :], D), ALU.mult), t)
            t = dve.do(lambda e: e.tensor_tensor(tmp[:, :, :], agg[:, :, :], over(w_agg[:, :], C7), ALU.mult), t)
            t2 = dve.do(lambda e, s=s: e.tensor_tensor(tmp2[:, :, :], s, over(w_skip[:, :], C7), ALU.mult), t_s[c])
            t = dve.do(lambda e: e.tensor_tensor(tmp[:, :, :], tmp[:, :, :], tmp2[:, :, :], ALU.add), t, t2)
            t = dve.do(lambda e, b=b: e.tensor_reduce(z[:, b, :], tmp[:, :, :], AX, ALU.add), t)
            t_g = act.do(lambda e, b=b: e.activation(z[:, b, :], z[:, b, :], ACT.Sigmoid, bias=bg[:, :]), t, t_w)
            t = dve.do(lambda e, s=s: e.tensor_tensor(tmp[:, :, :], s, agg[:, :, :], ALU.subtract), t)
            t_use[c] = t
            if c + 2 < W // C7:
                fetch(c + 2)
            t = dve.do(lambda e, b=b: e.tensor_tensor(tmp[:, :, :], tmp[:, :, :], wide(z[:, b, :], F), ALU.mult), t, t_g)
            t = dve.do(lambda e: e.tensor_tensor(agg[:, :, :], agg[:, :, :], tmp[:, :, :], ALU.add), t)
            t = normalize(k, agg[:, :, :], stats[:, :, :], moments[:, :, :], C7, [t])
            t = dve.do(lambda e: e.tensor_tensor(tmp[:, :, :], agg[:, :, :], wide(moments[:, :, 1], F), ALU.mult), t)
            t = dve.do(lambda e: e.tensor_tensor(tmp[:, :, :], tmp[:, :, :], wide(moments[:, :, 0], F), ALU.add), t)
            t = dve.do(lambda e: e.tensor_tensor(tmp[:, :, :], tmp[:, :, :], over(gamma[:, :], C7), ALU.mult), t)
            t = dve.do(lambda e: e.tensor_tensor(tmp[:, :, :], tmp[:, :, :], over(beta[:, :], C7), ALU.add), t)
            t = dve.do(lambda e: e.tensor_scalar(tmp2[:, :, :], tmp[:, :, :], 0.0, alpha[:, 0:1], ALU.min, ALU.mult), t)
            t = dve.do(lambda e: e.scalar_tensor_tensor(out=tmp[:, :, :], in0=tmp[:, :, :], scalar=0.0, in1=tmp2[:, :, :],
                                                        op0=ALU.max, op1=ALU.add), t)
            t = dve.do(lambda e, x=x: e.tensor_tensor(x, x, tmp[:, :, :], ALU.add), t)
        run_lanes(k)


def relation_tables(k):
    dve, act, pe, sp, a = k.dve, k.act, k.pe, k.sp, k.a
    with ExitStack() as ctx:
        sb = scratch(k, ctx)
        wr = sb("wr", [P, R, F])
        ws = sb("ws", [P, F])
        stats = sb("stats", [P, C7, 6])
        moments = sb("moments", [P, 2, C7, 2])
        seen = sb("seen", [P, W, R])
        h = sb("h", [P, 2, F])
        ht = sb("ht", [P, 2, F])
        xw = sb("xw", [P, 4, R * F])
        load_rows(k, [(wr[:, :, :], a["L1_gnn_weight"].rearrange("r i o -> i r o"))])
        t_w = load_rows(k, [(ws[:, :], a["L1_gnn_self_weight"])])
        cnt = k.inverse[:, 0:W, :]
        t = dve.do(lambda e: e.tensor_scalar(seen[:, :, :], cnt, 0.0, None, ALU.is_gt))
        t = dve.do(lambda e: e.tensor_scalar(cnt, cnt, 1.0, None, ALU.max), t)
        t = dve.do(lambda e: e.reciprocal(cnt, cnt), t)
        dve.do(lambda e: e.tensor_tensor(cnt, cnt, seen[:, :, :], ALU.mult), t)
        dve.do(lambda e: e.memset(k.inverse[:, W, :], 0.0))
        dve.do(lambda e: e.memset(k.acc[:, W, :], 0.0))
        xw_rows = k.table_xw.rearrange("(w p r) f -> w p (r f)", p=P, r=R)
        t_h, t_ht, t_pe, t_a, t_b, t_c, t_out = ({} for _ in range(7))
        got = lambda d, i: [d[i]] if i in d else []
        for c in range(W // C7):
            x = k.x[:, c * C7:(c + 1) * C7, :]
            t_n = normalize(k, x, stats[:, :, :], moments[:, c % 2, :, :], C7, [(dve.sem, dve.n), *got(t_h, (c - 1) * C7 - 1)])
            for i in range(C7):
                w = c * C7 + i
                b, s = w % 2, w % 4
                t_h[w] = act.do(lambda e, c=c, i=i, b=b, x=x: e.activation(
                    h[:, b, :], x[:, i, :], ACT.Relu, bias=moments[:, c % 2, i, 0:1], scale=moments[:, c % 2, i, 1:2]),
                    t_n, *got(t_ht, w - 2))
                t_ht[w] = turn_window(k, h[:, b, :], k.psum[b], ht[:, b, :], [t_h[w]], got(t_ht, w - 2), got(t_pe, w - 2))
                lo, hi, own = k.psum[2 + b], k.psum[4 + b], k.psum[6 + b]
                pe.do(lambda e, b=b, lo=lo: e.matmul(lo[:, :], ht[:, b, :], wr[:, 0:4, :].rearrange("p r f -> p (r f)"), start=True, stop=True),
                      t_ht[w], t_w, *got(t_a, w - 2))
                pe.do(lambda e, b=b, hi=hi: e.matmul(hi[:, :], ht[:, b, :], wr[:, 4:8, :].rearrange("p r f -> p (r f)"), start=True, stop=True),
                      *got(t_b, w - 2))
                t_pe[w] = pe.do(lambda e, b=b, own=own: e.matmul(own[:, 0:F], ht[:, b, :], ws[:, :], start=True, stop=True), *got(t_c, w - 2))
                t_a[w] = dve.do(lambda e, s=s, lo=lo: e.tensor_copy(xw[:, s, 0:4 * F], lo[:, :]), t_pe[w], *got(t_out, w - 4))
                t_b[w] = act.do(lambda e, s=s, hi=hi: e.copy(xw[:, s, 4 * F:8 * F], hi[:, :]), t_pe[w], *got(t_out, w - 4))
                t_c[w] = dve.do(lambda e, w=w, own=own: e.tensor_copy(k.acc[:, w, :], own[:, 0:F]))
                t_out[w] = sp.dma(lambda e, w=w, s=s: e.dma_start(xw_rows[w], xw[:, s, :]), k.qv_out[s], t_a[w], t_b[w])
        for s in range(4):
            sp.wait(k.qv_out[s].token)
        run_lanes(k)


def plain_table(k, sb, w0, n, ready, state):
    act, sp = k.act, k.sp
    c = state["c"]
    state["c"] += 1
    b = c % 2
    x = k.x[:, w0:w0 + n, :]
    h, stats, moments = state["h"], state["stats"], state["moments"]
    t = normalize(k, x, stats[:, b, :, :], moments[:, b, :, :], n, [*ready, *state["done"].get(c - 2, [])])
    for i in range(n):
        t_h = act.do(lambda e, i=i: e.activation(h[:, b, i, :], x[:, i, :], ACT.Relu, bias=moments[:, b, i, 0:1],
                                                 scale=moments[:, b, i, 1:2]), t, *state["done"].get(c - 2, []), *state["used"].get(c - 2, []))
    rows = k.table_h.rearrange("(w p) f -> p w f", p=P)
    t_o = sp.dma(lambda e: e.dma_start(rows[:, w0:w0 + n, :], h[:, b, 0:n, :]), k.x_in[b], t_h)
    state["done"][c] = [t_o, t_h]
    return h[:, b, :, :], t_h, c


def table_state(k, sb, n):
    return {"c": 0, "done": {}, "used": {}, "h": sb("h", [P, 2, n, F]), "stats": sb("stats", [P, 2, n, 6]), "moments": sb("moments", [P, 2, n, 2])}


def gine_tables(k):
    dve, sp = k.dve, k.sp
    with ExitStack() as ctx:
        sb = scratch(k, ctx)
        state = table_state(k, sb, C7)
        for c in range(W // C7):
            t = dve.do(lambda e, c=c: e.tensor_tensor(k.x[:, c * C7:(c + 1) * C7, :], k.x[:, c * C7:(c + 1) * C7, :],
                                                      k.acc[:, c * C7:(c + 1) * C7, :], ALU.add))
        t = dve.do(lambda e: e.memset(k.acc17[:, :, F:F + 17], 0.0), t)
        dve.do(lambda e: e.memset(k.acc17[:, 0:W, F:F + 1], 1.0), t)
        dve.do(lambda e: e.memset(k.acc17[:, 0:W, F + 1:F + 2], 4.0))
        t = dve.do(lambda e: e.memset(k.acc17[:, W, 0:F], 0.0))
        for c in range(W // C7):
            h, t_h, n = plain_table(k, sb, c * C7, C7, [t], state)
            t_u = dve.do(lambda e, c=c, h=h: e.tensor_copy(k.acc17[:, c * C7:(c + 1) * C7, 0:F], h), t_h)
            state["used"][n] = [t_u]
        sp.wait(k.x_in[0].token, k.x_in[1].token)
        run_lanes(k)


G4 = 4
BLOCKS = [(w, min(G4, W - w)) for w in range(0, W, G4)]


def column(ap, n):
    return ap.rearrange("(c p) -> p c", p=n)


def gine_end(k):
    dve, act, pe, sp, pool, a = k.dve, k.act, k.pe, k.sp, k.pool, k.a
    got = lambda d, i: [d[i]] if i in d else []
    with ExitStack() as ctx:
        sb = scratch(k, ctx)
        wc = sb("wc", [17, F])
        w1 = sb("w1", [P, 2 * F])
        w2 = sb("w2", [P, 2, F])
        b2 = sb("b2", [1, F])
        cols = sb("cols", [P, 3, 2])
        et = sb("et", [17, 2, G4 * P])
        aggt = sb("aggt", [P, 2, G4 * P])
        hid = sb("hid", [P, 2, 2, G4 * P])
        stats = sb("bn_stats", [P, 2, len(BLOCKS), 6])
        moments = sb("bn_moments", [P, 2, 2])
        hot = sb("relu", [P, 2, 2, G4 * P])
        state = table_state(k, sb, G4)
        with k.nc.allow_non_contiguous_dma(reason="three vectors of 256"):
            load_rows(k, [(cols[:, i, :], column(a[f"L2_gnn_{n}"], P)) for i, n in enumerate(("b1", "gamma", "beta"))])
            t_w = load_rows(k, [(wc[0:1, :], a["L2_gnn_b_edge"].rearrange("(a n) -> a n", a=1)), (wc[1:17, :], a["L2_gnn_W_edge"]),
                                (w1[:, :], a["L2_gnn_W1"]), (w2[:, :, :], a["L2_gnn_W2"].rearrange("(c p) f -> p c f", p=P)),
                                (b2[:, :], a["L2_gnn_b2"].rearrange("(a n) -> a n", a=1))])
            run_lanes(k)
        t_e, t_agg, t_hp, t_ev, t_out, t_st = ({} for _ in range(6))
        for j, (w0, n) in enumerate(BLOCKS):
            b = j % 2
            pe_e, pe_a = k.psum[b], k.psum[2 + b]
            m = n * P
            for i in range(n):
                t = pe.do(lambda e, i=i, w0=w0, p=pe_e: e.transpose(p[0:17, i * P:(i + 1) * P], k.acc17[:, w0 + i, F:F + 17], k.ident[:, :]), *got(t_e, j - 2))
            t_e[j] = act.do(lambda e, b=b, m=m, p=pe_e: e.copy(et[:, b, 0:m], p[0:17, 0:m]), t, *got(t_agg, j - 2))
            for i in range(n):
                pe.do(lambda e, i=i, w0=w0, p=pe_a: e.matmul(p[:, i * P:(i + 1) * P], k.acc17[:, w0 + i, 0:F], k.ident[:, :], start=True, stop=False), *got(t_agg, j - 2))
                t = pe.do(lambda e, i=i, b=b, p=pe_a: e.matmul(p[:, i * P:(i + 1) * P], wc[:, :], et[:, b, i * P:(i + 1) * P], start=False, stop=True), t_e[j], t_w)
            t_agg[j] = dve.do(lambda e, b=b, m=m, p=pe_a: e.tensor_copy(aggt[:, b, 0:m], p[:, 0:m]), t, *got(t_hp, j - 2))
            for c in range(2):
                t_hp[j] = pe.do(lambda e, b=b, c=c, m=m: e.matmul(k.psum[4 + 2 * b + c][:, 0:m], w1[:, c * F:(c + 1) * F], aggt[:, b, 0:m], start=True, stop=True),
                                t_agg[j], *got(t_ev, j - 2))
            for c in range(2):
                t_ev[j] = act.do(lambda e, b=b, c=c, m=m: e.activation(hid[:, b, c, 0:m], k.psum[4 + 2 * b + c][:, 0:m], ACT.Identity, bias=cols[:, 0, c:c + 1]),
                                 t_hp[j], *got(t_out, j - 2), *got(t_st, j - 2))
            real = m if w0 + n < W else m - P + LAST
            for c in range(2):
                t_st[j] = dve.do(lambda e, j=j, b=b, c=c, real=real: e.bn_stats(stats[:, c, j, :], hid[:, b, c, 0:real]), t_ev[j])
            t_out[j] = sp.dma(lambda e, b=b, w0=w0, m=m: e.dma_start(k.hidden[:, :, w0 * P:w0 * P + m], hid[:, b, :, 0:m]), k.qv_out[b], t_ev[j])
        sp.wait(k.qv_out[0].token, k.qv_out[1].token)
        for c in range(2):
            t = dve.do(lambda e, c=c: e.bn_aggr(moments[:, c, :], stats[:, c, :, :].rearrange("p j s -> p (j s)")), t_st[len(BLOCKS) - 1])
        t = root(k, moments[:, :, 1], t)
        t = dve.do(lambda e: e.tensor_tensor(moments[:, :, 1], moments[:, :, 1], cols[:, 1, :], ALU.mult), t)
        t = dve.do(lambda e: e.tensor_tensor(moments[:, :, 0], moments[:, :, 0], moments[:, :, 1], ALU.mult), t)
        t_bn = dve.do(lambda e: e.tensor_tensor(moments[:, :, 0], cols[:, 2, :], moments[:, :, 0], ALU.subtract), t)
        run_lanes(k)

        t_z = dve.do(lambda e: e.memset(k.acc_flat[:, :], 0.0))
        t_in, t_r, t_o, t_x = ({} for _ in range(4))

        def fetch(j):
            w0, n = BLOCKS[j]
            t_in[j] = sp.dma(lambda e: e.dma_start(hid[:, j % 2, :, 0:n * P], k.hidden[:, :, w0 * P:(w0 + n) * P]), k.qv_out[2 + j % 2], *got(t_r, j - 2))
        fetch(0)
        for j, (w0, n) in enumerate(BLOCKS):
            b, m = j % 2, n * P
            if j + 1 < len(BLOCKS):
                fetch(j + 1)
            for c in range(2):
                t_r[j] = act.do(lambda e, b=b, c=c, m=m: e.activation(hot[:, b, c, 0:m], hid[:, b, c, 0:m], ACT.Relu, bias=moments[:, c, 0:1], scale=moments[:, c, 1:2]),
                                t_in[j], t_bn, *got(t_o, j - 2))
            for i in range(n):
                for c in range(2):
                    pe.do(lambda e, i=i, c=c, b=b: e.matmul(k.psum[b][:, i * P:(i + 1) * P], hot[:, b, c, i * P:(i + 1) * P], w2[:, c, :], start=(c == 0), stop=False),
                          t_r[j], *got(t_x, j - 2))
                t_o[j] = pe.do(lambda e, i=i, b=b: e.matmul(k.psum[b][:, i * P:(i + 1) * P], k.ones[0:1, :], b2[:, :], start=False, stop=True))
            t_x[j] = dve.do(lambda e, w0=w0, n=n, b=b, m=m: e.tensor_tensor(k.x[:, w0:w0 + n, :], k.x[:, w0:w0 + n, :],
                            k.psum[b][:, 0:m].rearrange("p (n f) -> p n f", f=F), ALU.add), t_o[j])
            plain_table(k, sb, w0, n, [t_x[j]], state)
        sp.wait(k.x_in[0].token, k.x_in[1].token)
        run_lanes(k)


def edge_conv_end(k):
    dve, act, pe, sp, a = k.dve, k.act, k.pe, k.sp, k.a
    got = lambda d, i: [d[i]] if i in d else []
    with ExitStack() as ctx:
        sb = scratch(k, ctx)
        wc = sb("wc", [7, F])
        be = sb("be", [1, F])
        w3 = sb("w3", [P, F])
        et = sb("et", [7, 2, G4 * P])
        aggt = sb("aggt", [P, 2, G4 * P])
        out = sb("out_sb", [P, 2, G4, F])
        vec = lambda n: a[n].rearrange("(a n) -> a n", a=1)
        t_w = load_rows(k, [(wc[0:1, :], vec("L3_gnn_b")), (wc[1:7, :], a["L3_gnn_We"]), (be[:, :], vec("L3_gnn_be")), (w3[:, :], a["L3_gnn_W"])])
        t_wc = dve.do(lambda e: e.tensor_tensor(wc[0:1, :], wc[0:1, :], be[:, :], ALU.add), t_w)
        t_e, t_agg, t_o, t_x, t_out = ({} for _ in range(5))
        rows = k.out.rearrange("(w p) f -> p w f", p=P)
        for j, (w0, n) in enumerate(BLOCKS):
            b, m = j % 2, n * P
            for i in range(n):
                t = pe.do(lambda e, i=i, w0=w0, b=b: e.transpose(k.psum[b][0:7, i * P:(i + 1) * P], k.acc7[:, w0 + i, F:F + 7], k.ident[:, :]), *got(t_e, j - 2))
            t_e[j] = act.do(lambda e, b=b, m=m: e.copy(et[:, b, 0:m], k.psum[b][0:7, 0:m]), t, *got(t_o, j - 2))
            for i in range(n):
                t = pe.do(lambda e, i=i, w0=w0, b=b: e.transpose(k.psum[2 + b][:, i * P:(i + 1) * P], k.acc7[:, w0 + i, 0:F], k.ident[:, :]), *got(t_agg, j - 2))
            t_agg[j] = act.do(lambda e, b=b, m=m: e.copy(aggt[:, b, 0:m], k.psum[2 + b][:, 0:m]), t, *got(t_o, j - 2))
            for i in range(n):
                pe.do(lambda e, i=i, b=b: e.matmul(k.psum[4 + b][:, i * P:(i + 1) * P], aggt[:, b, i * P:(i + 1) * P], w3[:, :], start=True, stop=False),
                      t_agg[j], t_e[j], t_wc, *got(t_x, j - 2))
                t_o[j] = pe.do(lambda e, i=i, b=b: e.matmul(k.psum[4 + b][:, i * P:(i + 1) * P], et[:, b, i * P:(i + 1) * P], wc[:, :], start=False, stop=True))
            t_x[j] = dve.do(lambda e, w0=w0, n=n, b=b, m=m: e.scalar_tensor_tensor(
                out=out[:, b, 0:n, :], in0=k.psum[4 + b][:, 0:m].rearrange("p (n f) -> p n f", f=F), scalar=0.0,
                in1=k.x[:, w0:w0 + n, :], op0=ALU.max, op1=ALU.add), t_o[j], *got(t_out, j - 2))
            t_out[j] = sp.dma(lambda e, w0=w0, n=n, b=b: e.dma_start(rows[:, w0:w0 + n, :], out[:, b, 0:n, :]), k.x_in[b], t_x[j])
        sp.wait(k.x_in[0].token, k.x_in[1].token)
        run_lanes(k)


def layers(k, upto=99):
    nc = k.nc
    counters = lambda name, n: [Counter(k.sem(f"s_{name}{i}")) for i in range(n)]
    k.x_in, k.qv_out, k.skip_out = counters("x_in", 2), counters("qv_out", 4), counters("skip_out", 4)
    k.t_qv, k.t_skip = {}, {}
    dram = lambda name, shape: nc.dram_tensor(name, shape, F32).ap()
    k.table_qv = dram("table_qv", [NP, 2 * F])
    k.table_xw = dram("table_xw", [NP * R, F])
    k.table_h = dram("table_h", [NP, F])
    k.skip = dram("skip_rows", [P, W, F])
    k.hidden = dram("hidden", [P, 2, NP])
    k.acc_flat = k.sb("acc", [P, (W + 1) * (F + 17)])
    part = lambda n: k.acc_flat[:, 0:(W + 1) * n].rearrange("p (w n) -> p w n", n=n)
    k.acc, k.acc17, k.acc7 = part(F), part(F + 17), part(F + 7)
    attn = part(H * (D + 1))
    k.x = k.sb("x", [P, W + 1, F])
    k.keys = k.x
    k.inverse = k.sb("inverse", [P, W + 1, R])
    top = k.sb("top", [P, W + 1, H])
    k.pool.do(lambda e: e.memset(k.inverse[:, :, :], 0.0))
    k.pool.do(lambda e: e.memset(top[:, :, :], NONE))
    k.pool.do(lambda e: e.memset(k.acc_flat[:, :], 0.0))
    attention_tables(k)
    if upto == 2:
        return
    count_pass(k, k.rec_src, CS, k.win_src, k.inverse)
    if upto == 3:
        return
    attention_pass(k, k.rec_dst, CD, k.win_dst, k.table_qv, k.keys, top, attn, k.inverse)
    attention_end(k)
    if upto == 4:
        return
    relation_tables(k)
    relation_pass(k, k.rec_dst, CD, k.win_dst, k.table_xw, k.acc)
    relation_pass(k, k.rec_src, CS, k.win_src, k.table_xw, k.acc)
    if upto == 5:
        return
    gine_tables(k)
    sum_pass(k, k.rec_src, CS, k.win_src, k.table_h, k.acc17, 17)
    if upto == 6:
        return
    gine_end(k)
    sum_pass(k, k.rec_dst, CD, k.win_dst, k.table_h, k.acc7, 7)
    edge_conv_end(k)


_EDGE = ("src", "dst", "edge_type_8", "edge_attr_16", "edge_attr_6")


def kernel(**inputs):
    import concourse.bacc as bacc
    from concourse.bass_utils import run_bass_kernel_spmd

    nc = bacc.Bacc("TRN2", target_bir_lowering=False, num_devices=1)
    arrays, aps = {}, {}
    for name, a in inputs.items():
        a = np.asarray(a)
        if name in _EDGE:
            fill = np.full((ET * P - E, *a.shape[1:]), N if name in ("src", "dst") else 0, a.dtype)
            a = np.concatenate([a, fill])
        if name == "x":
            a = np.concatenate([a, np.zeros((NP - N, F), a.dtype)])
        if a.ndim == 0:
            a = a.reshape(1)
        a = np.ascontiguousarray(a)
        arrays[f"in_{name}"] = a
        aps[name] = nc.dram_tensor(f"in_{name}", a.shape, mybir.dt.from_np(a.dtype), kind="ExternalInput").ap()
    out = nc.dram_tensor("out", [NP, F], F32, kind="ExternalOutput").ap()
    build_program(nc, aps, out)
    result = run_bass_kernel_spmd(nc, [arrays], core_ids=[0])
    return result.results[0]["out"][:N]
```

```python
from contextlib import ExitStack

import numpy as np

import concourse.bass as bass
from concourse import mybir
from concourse.alu_op_type import AluOpType as ALU

P = 128
F = 128
N = 12500
E = 200000
R = 8
H = 4
D = F // H
W = -(-N // P)
NP = W * P
ET = -(-E // P)
LAST = N - (W - 1) * P

GT = 4
BODY = 16
RING = 8
NREC = 4
RG = 4
TILES = -(-(ET * P + W * (P - 1)) // P)
GROUPS = -(-TILES // (GT * BODY)) * BODY
NT = GROUPS * GT
LEAD = 3
TP = NT + 2 * RG * GT
CH = 32
CHUNKS = -(-ET // CH)

IDX, IDX8, LOC, TYP, ONE, ATT = range(6)
CD = ATT + 6
CS = ATT + 16

CREDIT = 32
NONE = -1.0e30
EPS = 1e-5

F32, BF16, I32, I16 = mybir.dt.float32, mybir.dt.bfloat16, mybir.dt.int32, mybir.dt.int16
ACT = mybir.ActivationFunctionType
AX = mybir.AxisListType.X


class Lane:

    def __init__(self, sem):
        self.sem, self.n, self.ops, self.seen = sem, 0, [], {}

    def wait(self, *tokens):
        for sem, value in tokens:
            if self.seen.get(id(sem), 0) < value:
                self.seen[id(sem)] = value
                self.ops.append(lambda e, s=sem, v=value: e.wait_ge(s, v))

    def do(self, what, *tokens):
        self.wait(*tokens)
        self.n += 1
        self.ops.append(lambda e, s=self.sem: what(e).then_inc(s, 1))
        return self.sem, self.n

    def dma(self, what, counter, *tokens):
        self.wait(*tokens)
        counter.n += 16
        self.ops.append(lambda e, s=counter.sem: what(e).then_inc(s, 16))
        return counter.sem, counter.n

    def play(self, engine):
        for op in self.ops:
            op(engine)
        self.ops = []


class Counter:
    def __init__(self, sem):
        self.sem, self.n = sem, 0

    @property
    def token(self):
        return self.sem, self.n


class Turn:

    def __init__(self, e, value, phase):
        self.e, self.value, self.times, self.phase = e, value, {}, phase
        self.sum = e.alloc_register(f"sum_{phase}")

    def multiple(self, per):
        if per not in self.times:
            self.times[per] = self.e.alloc_register(f"turn_{per}_{self.phase}")
            self.e.reg_mul(self.times[per], self.e.to_reg(self.value), per)
        return self.times[per]

    def close(self):
        for r in (self.sum, *self.times.values()):
            self.e.free_register(r)


class Group:

    def __init__(self, turn, j):
        self.turn, self.n, self.j = turn, j, j % BODY

    def count(self, sem, per, every, more):
        return sem, self.turn, BODY // every * per, self.n // every * per + more

    def tile(self, k):
        number = self.n * GT + k
        return self.turn.value * (BODY * GT) + number if self.turn else number


def until(e, mark):
    sem, turn, per, more = mark
    if turn is None:
        e.wait_ge(sem, more)
    else:
        e.reg_add(turn.sum, turn.multiple(per), more)
        e.wait_ge(sem, turn.sum)


def wide(ap, n):
    return ap.unsqueeze(2).to_broadcast([ap.shape[0], ap.shape[1], n])


def over(ap, m):
    return ap.unsqueeze(1).to_broadcast([ap.shape[0], m, ap.shape[1]])


class Core:
    pass


def build_program(nc, a, out):
    ctx = ExitStack()
    with ctx:
        k = Core()
        k.nc, k.a, k.out = nc, a, out
        k.phase = 0
        k.sem = lambda name: ctx.enter_context(nc.semaphore(name))
        k.sb = scratch(k, ctx)
        k.dve, k.act, k.pe, k.pool, k.sp = (Lane(k.sem(f"s_{n}")) for n in ("dve", "act", "pe", "pool", "sp"))
        k.load = Counter(k.sem("s_load"))
        k.store = Counter(k.sem("s_store"))
        k.rec_dst = nc.dram_tensor("rec_dst", [P, TP, CD], F32).ap()
        k.raw_src = nc.dram_tensor("raw_src", [P, ET, CS], F32).ap()
        k.rec_src = nc.dram_tensor("rec_src", [P, TP, CS], F32).ap()
        k.banks = ctx.enter_context(nc.psum_tensor("banks", [P, 8, 512], F32))
        k.psum = [k.banks[:, i, :] for i in range(8)]
        k.win_dst = k.sb("win_dst", [1, TP], I32)
        k.win_src = k.sb("win_src", [1, TP], I32)
        k.row_src = k.sb("row_src", [P, ET], I32)
        dram_tables(k)
        k.ring_sem = [k.sem(f"s_ring{i}") for i in range(RING)]
        k.ring_base = [0] * RING
        k.rec_sem = [k.sem(f"s_rec{i}") for i in range(NREC)]
        k.rec_base = [0] * NREC
        k.pass_sem, k.pass_base = {}, {}
        constants(k)
        sort_edges(k)
        layers(k)


def scratch(k, ctx):
    k.phase += 1
    return lambda name, shape, dt=F32, n=k.phase: ctx.enter_context(k.nc.sbuf_tensor(f"{name}_{n}", shape, dt))


def run_lanes(k):
    with k.nc.Block() as block:
        block.sync(lambda e: k.sp.play(e))
        block.gpsimd(lambda e: k.pool.play(e))
        block.scalar(lambda e: k.act.play(e))
        block.vector(lambda e: k.dve.play(e))
        block.tensor(lambda e: k.pe.play(e))


def constants(k):
    pool, dve = k.pool, k.dve
    k.col_i = k.sb("col_i", [P, P], I32)
    k.col = k.sb("col", [P, P])
    k.ident = k.sb("ident", [P, P])
    k.ident_b = k.sb("ident_b", [P, P], BF16)
    k.none4 = k.sb("none4", [P, H, P], BF16)
    k.ones = k.sb("ones", [P, P])
    k.before = k.sb("before", [P, P])
    t_col = pool.do(lambda e: e.iota(k.col_i[:, :], [[1, P]], base=0, channel_multiplier=0))
    t_one = pool.do(lambda e: e.memset(k.ones[:, :], 1.0))
    t_z = pool.do(lambda e: e.memset(k.ident[:, :], 0.0))
    t_id = pool.do(lambda e: e.affine_select(out=k.ident[:, :], in_=k.ident[:, :], compare_op=ALU.not_equal,
                                             fill=1.0, base=0, pattern=[[-1, P]], channel_multiplier=1), t_z)
    t_tri = pool.do(lambda e: e.affine_select(out=k.before[:, :], in_=k.ones[:, :], compare_op=ALU.is_ge,
                                              fill=0.0, base=-1, pattern=[[1, P]], channel_multiplier=-1), t_one)
    dve.do(lambda e: e.tensor_copy(k.col[:, :], k.col_i[:, :]), t_col)
    t_ib = dve.do(lambda e: e.tensor_copy(k.ident_b[:, :], k.ident[:, :]), t_id)
    dve.do(lambda e: e.tensor_scalar(k.none4[:, :, :], over(k.ident_b[:, :], H), NONE, None, ALU.mult), t_ib, t_tri)
    run_lanes(k)


def sort_edges(k):
    nc, dve, act, pe, pool, sp = k.nc, k.dve, k.act, k.pe, k.pool, k.sp
    with ExitStack() as ctx:
        sb = scratch(k, ctx)
        typ_i = sb("typ_i", [P, ET], I32)
        typ = sb("typ", [P, ET])
        node_i = {s: sb(f"node_{s}", [P, ET], I32) for s in ("src", "dst")}
        idx8 = {s: sb(f"idx8_{s}", [P, ET], I32) for s in ("src", "dst")}
        loc = {s: sb(f"loc_{s}", [P, ET]) for s in ("src", "dst")}
        row = {"dst": sb("row_dst", [P, ET], I32), "src": k.row_src}
        tmp_i = sb("tmp_i", [P, ET], I32)
        win = sb("win", [P, ET], BF16)
        hit = sb("hit", [P, 2, ET], BF16)
        rank = sb("rank", [P, 2, ET])
        slot = sb("slot", [P, ET])
        count = sb("count", [P, W])
        total = sb("total", [P, W])
        tiles_i = sb("tiles_i", [P, W], I32)
        tiles = sb("tiles", [P, W])
        ends = sb("ends", [P, W])
        base = sb("base", [P, W])
        end_col = sb("end_col", [W, 1])
        step_i = sb("step_i", [W, TP], I32)
        passed = sb("passed", [W, TP])
        blank = {"dst": sb("blank_d", [P, RG * GT, CD]), "src": sb("blank_s", [P, RG * GT, CS])}
        att = {"dst": sb("att_d", [P, 2, CH, CD - ATT]), "src": sb("att_s", [P, 2, CH, CS - ATT])}
        stage = {"dst": sb("stage_d", [P, 2, CH, CD]), "src": sb("stage_s", [P, 2, CH, CS])}
        rec = {"dst": k.rec_dst, "src": k.rec_src}
        windows = {"dst": k.win_dst, "src": k.win_src}
        s_att = {s: [Counter(k.sem(f"s_att_{s}{i}")) for i in range(2)] for s in ("src", "dst")}
        s_out = {s: [Counter(k.sem(f"s_out_{s}{i}")) for i in range(2)] for s in ("src", "dst")}
        tables = attention_tables(k, sb)
        next(tables)
        s_fill = {s: Counter(k.sem(f"s_fill_{s}")) for s in ("src", "dst")}

        for name, to in (("src", node_i["src"]), ("dst", node_i["dst"]), ("edge_type_8", typ_i)):
            t_in = sp.dma(lambda e, n=name, to=to: e.dma_start(to[:, :], k.a[n].rearrange("(p t) -> p t", p=P)), k.load)

        t_fill = {}
        for s in ("dst", "src"):
            t = pool.do(lambda e, s=s: e.memset(blank[s][:, :, :], 0.0))
            t = pool.do(lambda e, s=s: e.memset(blank[s][:, :, LOC:LOC + 1], -1.0), t)
            for b in range(0, TP, RG * GT):
                t_fill[s] = sp.dma(lambda e, s=s, b=b: e.dma_start(rec[s][:, b:b + RG * GT, :], blank[s][:, :, :]), s_fill[s], t)
        t_step = pool.do(lambda e: e.iota(step_i[:, :], [[1, TP]], base=0, channel_multiplier=0))
        t_st = {}
        for s in ("src", "dst"):
            t_st[s] = pool.do(lambda e, s=s: e.memset(stage[s][:, :, :, :], 1.0))

        t_typ = dve.do(lambda e: e.tensor_copy(typ[:, :], typ_i[:, :]), t_in)
        t_row, t_ready = {}, {}
        t_prev = None
        for s in ("dst", "src"):
            far = "dst" if s == "src" else "src"
            t = dve.do(lambda e, s=s: e.tensor_scalar(tmp_i[:, :], node_i[s][:, :], 7, None, ALU.arith_shift_right), *([t_prev] if t_prev else []))
            t = dve.do(lambda e: e.tensor_copy(win[:, :], tmp_i[:, :]), t)
            t = dve.do(lambda e, s=s: e.tensor_scalar(tmp_i[:, :], node_i[s][:, :], P - 1, None, ALU.bitwise_and), t)
            dve.do(lambda e, s=s: e.tensor_copy(loc[s][:, :], tmp_i[:, :]), t)
            t = dve.do(lambda e, s=s, f=far: e.scalar_tensor_tensor(out=idx8[s][:, :], in0=node_i[f][:, :], scalar=float(R),
                                                                    in1=typ_i[:, :], op0=ALU.mult, op1=ALU.add))
            for w in range(W):
                t = dve.do(lambda e, w=w: e.tensor_scalar(hit[:, w % 2, :], win[:, :], float(w), 0.0, ALU.is_equal, ALU.add,
                                                          accum_out=count[:, w:w + 1]), *([t] if w < 2 else [t_b[w % 2]]))
                t_b = [t, t] if w == 0 else [t if w % 2 == i else t_b[i] for i in range(2)]
            pt, pb = k.psum[0], k.psum[1]
            t_t = pe.do(lambda e: e.matmul(pt[:, 0:W], k.ones[:, :], count[:, :], start=True, stop=True), t, (dve.sem, dve.n))
            t_p = pe.do(lambda e: e.matmul(pb[:, 0:W], k.before[:, :], count[:, :], start=True, stop=True))
            t = dve.do(lambda e: e.tensor_scalar(total[:, :], pt[:, 0:W], float(P - 1), None, ALU.add), t_t)
            t = dve.do(lambda e: e.tensor_copy(tiles_i[:, :], total[:, :]), t)
            t = dve.do(lambda e: e.tensor_scalar(tiles_i[:, :], tiles_i[:, :], 7, None, ALU.arith_shift_right), t)
            t = dve.do(lambda e: e.tensor_copy(tiles[:, :], tiles_i[:, :]), t)
            t_e = dve.do(lambda e: e.tensor_tensor_scan(ends[:, :], tiles[:, :], tiles[:, :], 0.0, ALU.add, ALU.bypass), t)
            t = dve.do(lambda e: e.tensor_tensor(base[:, :], ends[:, :], tiles[:, :], ALU.subtract), t_e)
            t = dve.do(lambda e: e.tensor_scalar(base[:, :], base[:, :], float(P), -1.0, ALU.mult, ALU.add), t)
            t = dve.do(lambda e: e.tensor_tensor(base[:, :], base[:, :], pb[:, 0:W], ALU.add), t, t_p)
            t_h, t_k, t_s = [t, t], [t, t], [t, t]
            for w in range(W):
                b = w % 2
                t_h[b] = dve.do(lambda e, w=w, b=b: e.tensor_scalar(hit[:, b, :], win[:, :], float(w), None, ALU.is_equal), t_s[b])
                t_k[b] = dve.do(lambda e, w=w, b=b: e.tensor_tensor_scan(rank[:, b, :], hit[:, b, :], hit[:, b, :], base[:, w:w + 1],
                                                                         ALU.add, ALU.bypass), t_h[b])
                t_s[b] = dve.do(lambda e, w=w, b=b: e.copy_predicated(slot[:, :], hit[:, b, :].bitcast(I16), rank[:, b, :]),
                                t_k[b], t_s[1 - b])
            t = dve.do(lambda e, s=s: e.tensor_copy(row[s][:, :], slot[:, :]), t_s[0], t_s[1])
            t = dve.do(lambda e, s=s: e.tensor_scalar(tmp_i[:, :], row[s][:, :], 7, None, ALU.arith_shift_right), t)
            t = dve.do(lambda e, s=s: e.tensor_scalar(row[s][:, :], row[s][:, :], P - 1, None, ALU.bitwise_and), t)
            t_row[s] = t_prev = dve.do(lambda e, s=s: e.scalar_tensor_tensor(out=row[s][:, :], in0=row[s][:, :], scalar=float(TP),
                                                                    in1=tmp_i[:, :], op0=ALU.mult, op1=ALU.add), t)
            t_tr = pe.do(lambda e: e.transpose(pt[0:W, 0:P], ends[:, :], k.ident[:, :]), t_e, t_t)
            t = dve.do(lambda e: e.tensor_copy(end_col[:, :], pt[0:W, 0:1]), t_tr)
            t = dve.do(lambda e: e.tensor_scalar(passed[:, :], step_i[:, :], end_col[:, 0:1], None, ALU.is_ge), t, t_step)
            for c in range(0, TP, 512):
                n = min(512, TP - c)
                t_w = pe.do(lambda e, c=c, n=n: e.matmul(k.psum[2][0:1, 0:n], k.ones[0:W, 0:1], passed[:, c:c + n], start=True, stop=True), t, t_prev)
                t_prev = dve.do(lambda e, c=c, n=n, s=s: e.tensor_copy(windows[s][:, c:c + n], k.psum[2][0:1, 0:n]), t_w)
                t = t_prev

        t_cp, t_out = {}, {}

        def stage_records(s, j):
            far, b, c = "dst" if s == "src" else "src", j % 2, j * CH
            n = min(CH, ET - c)
            attr = k.a["edge_attr_16" if s == "src" else "edge_attr_6"].rearrange("(p t) c -> p t c", p=P)
            old = [t_cp[s, j - 2]] if j > 1 else []
            t_a = sp.dma(lambda e: e.dma_start(att[s][:, b, 0:n, :], attr[:, c:c + n, :]), s_att[s][b], *old)
            wait = [t_st[s], t_row[s]] + ([t_out[s, j - 2]] if j > 1 else [])
            act.do(lambda e: e.copy(stage[s][:, b, 0:n, IDX].bitcast(I32), node_i[far][:, c:c + n]), *wait)
            act.do(lambda e: e.copy(stage[s][:, b, 0:n, IDX8].bitcast(I32), idx8[s][:, c:c + n]))
            act.do(lambda e: e.copy(stage[s][:, b, 0:n, LOC], loc[s][:, c:c + n]))
            act.do(lambda e: e.copy(stage[s][:, b, 0:n, TYP], typ[:, c:c + n]), t_typ)
            t_cp[s, j] = act.do(lambda e: e.copy(stage[s][:, b, 0:n, ATT:], att[s][:, b, 0:n, :]), t_a)
            return b, c, n

        flat = k.rec_dst.rearrange("p t c -> (p t) c")
        windows_done = 0
        first = CHUNKS * 3 // 10
        for j in range(CHUNKS):
            b, c, n = stage_records("dst", j)
            for i in range(n):
                t_out["dst", j] = pool.dma(lambda e, b=b, i=i, c=c: e.indirect_dma_start(
                    out=flat, out_offset=bass.IndirectOffsetOnAxis(ap=row["dst"][:, c + i:c + i + 1], axis=0),
                    in_=stage["dst"][:, b, i, :], in_offset=None), s_out["dst"][b], t_cp["dst", j], t_fill["dst"])
            if j < first:
                continue
            for m in range(CHUNKS * (j - first) // (CHUNKS - first), CHUNKS * (j + 1 - first) // (CHUNKS - first)):
                b, c, n = stage_records("src", m)
                t_out["src", m] = sp.dma(lambda e, b=b, c=c, n=n: e.dma_start(k.raw_src[:, c:c + n, :], stage["src"][:, b, 0:n, :]),
                                         s_out["src"][b], t_cp["src", m])
            if j == first:
                pe.wait(t_prev)
            while windows_done < W * (j + 1 - first) // (CHUNKS - first):
                next(tables)
                windows_done += 1
        next(tables)
        pool.wait(*(c.token for c in s_out["dst"]))
        sp.wait(*(c.token for c in s_out["src"]), t_fill["src"])
        run_lanes(k)


class SourceRecords:

    def __init__(self, k, sb):
        self.k, self.n = k, RG * GT
        self.blocks = -(-ET // self.n)
        self.buffer = sb("moved", [P, NREC, self.n, CS])
        self.s_in = [k.sem(f"s_raw_in{i}") for i in range(NREC)]
        self.s_out = [k.sem(f"s_raw_out{i}") for i in range(NREC)]
        self.target = k.rec_src.rearrange("p t c -> (p t) c")

    def tiles(self, c):
        return min(self.n, ET - c * self.n)

    def load(self, e, c):
        if c < self.blocks:
            b = c % NREC
            if c >= NREC:
                e.wait_ge(self.s_out[b], 16 * self.n * (c // NREC))
            n = self.tiles(c)
            e.dma_start(self.buffer[:, b, 0:n, :], self.k.raw_src[:, c * self.n:c * self.n + n, :]).then_inc(self.s_in[b], 16)

    def scatter(self, e, g):
        c, first = g // RG, g % RG * GT
        if c < self.blocks:
            b = c % NREC
            if first == 0:
                e.wait_ge(self.s_in[b], 16 * (c // NREC + 1))
            for i in range(first, min(first + GT, self.tiles(c))):
                t = c * self.n + i
                e.indirect_dma_start(out=self.target, out_offset=bass.IndirectOffsetOnAxis(ap=self.k.row_src[:, t:t + 1], axis=0),
                                     in_=self.buffer[:, b, i, :], in_offset=None).then_inc(self.s_out[b], 16)

    def finish(self, e):
        for b in range(NREC):
            e.wait_ge(self.s_out[b], 16 * sum(self.tiles(c) for c in range(b, self.blocks, NREC)))


class Pass:

    def __init__(self, k, rec, cols, win, row, leads):
        self.k, self.rec, self.cols, self.win, self.row, self.leads = k, rec, cols, win, row, leads
        self.stages = {e: [] for e in ("vector", "scalar", "tensor")}
        self.per = {}
        self.credit = []
        self.leads_of = {}

    def at(self, name, group, nth=None):
        per = self.per[name]
        more = (per if nth is None else nth) + self.k.pass_base.get(name, 0)
        return group.count(self.k.pass_sem[name], per, 1, more)

    def at_before(self, name, group, depth, nth=None):
        sem, turn, per, more = self.at(name, group, nth)
        more -= depth * self.per[name]
        if turn is None:
            more = max(more, self.k.pass_base[name])
        return sem, turn, per, more

    def record(self, group):
        b = group.j // RG % NREC
        return group.count(self.k.rec_sem[b], 16, RG * NREC, 16 + self.k.rec_base[b])

    def gathered(self, group):
        b = group.j % RING
        return group.count(self.k.ring_sem[b], 16 * GT, RING, 16 * GT + self.k.ring_base[b])

    def rows(self, group, lo, hi):
        b = group.j // RG % NREC
        t = group.j % RG * GT
        return self.recs[:, b, t:t + GT, lo:hi]

    def stage(self, engine, name, per, lead, work):
        self.per[name] = per
        self.k.pass_sem.setdefault(name, None)
        if self.k.pass_sem[name] is None:
            self.k.pass_sem[name] = self.k.sem(f"p_{name}")
            self.k.pass_base[name] = CREDIT
            self.credit.append((engine, name))
        self.stages[engine].append((lead, name, work))
        self.leads_of[name] = lead

    def run(self, table, gather_lead, freed, last, beside=None):
        k = self.k
        blocks = TP // (RG * GT)
        gathers = GROUPS + gather_lead if table is not None else 0

        def play(engine, e):
            for owner, name in self.credit:
                if owner == engine:
                    e.sem_inc(k.pass_sem[name], CREDIT)
            for step in range(-self.leads, 0):
                for lead, _, work in self.stages[engine]:
                    if step + lead >= 0:
                        work(e, Group(None, step + lead))
            with e.Fori(0, GROUPS // BODY) as value:
                turn = Turn(e, value, k.phase)
                for j in range(BODY):
                    for lead, _, work in self.stages[engine]:
                        work(e, Group(turn, j + lead))
                turn.close()

        def sync(e):
            for c in range(blocks):
                if c >= NREC:
                    until(e, self.at(last, Group(None, (c - NREC) * RG + RG - 1)))
                e.dma_start(self.recs[:, c % NREC, :, :],
                            self.rec[:, c * RG * GT:(c + 1) * RG * GT, :]).then_inc(k.rec_sem[c % NREC], 16)
                if beside:
                    beside.load(e, c)
            for b in range(NREC):
                n = len(range(b, blocks, NREC))
                k.rec_base[b] += 16 * n
                e.wait_ge(k.rec_sem[b], k.rec_base[b])

        def gpsimd(e):
            for g in range(gathers):
                group = Group(None, g)
                if g % RG == 0:
                    until(e, self.record(group))
                if g >= RING:
                    until(e, self.at(freed, Group(None, g - RING)))
                for t in range(GT):
                    index = self.rows(group, self.row, self.row + 1)[:, t, :].bitcast(I32)
                    e.indirect_dma_start(out=self.far[:, g % RING, t, :], out_offset=None, in_=table,
                                         in_offset=bass.IndirectOffsetOnAxis(ap=index, axis=0)
                                         ).then_inc(k.ring_sem[g % RING], 16)
                if beside:
                    beside.scatter(e, g)
            if beside:
                beside.finish(e)
            for b in range(RING):
                if gathers:
                    e.wait_ge(k.ring_sem[b], k.ring_base[b] + 16 * GT * len(range(b, gathers, RING)))

        with k.nc.Block() as block:
            block.gpsimd(gpsimd)
            block.vector(lambda e: play("vector", e))
            block.scalar(lambda e: play("scalar", e))
            block.tensor(lambda e: play("tensor", e))
            block.sync(sync)
        for b in range(RING):
            k.ring_base[b] += 16 * GT * len(range(b, gathers, RING))
        for name, lead in self.leads_of.items():
            k.pass_base[name] += (GROUPS + lead) * self.per[name]


def count_pass(k, rec, cols, win):
    with ExitStack() as ctx:
        sb = scratch(k, ctx)
        ps = Pass(k, rec, cols, win, IDX, LEAD)
        ps.recs = sb("recs", [P, NREC, RG * GT, cols])
        hot = sb("hot", [P, NREC, RG * GT, P], BF16)
        kind = sb("kind", [P, NREC, RG * GT, R], BF16)
        totals = totals_of(k)
        at = []

        def mark(e, g):
            if g.j % RG:
                return
            b, n = g.j // RG % NREC, RG * GT
            until(e, ps.record(g))
            until(e, ps.at_before("count", g, NREC * RG - RG + 1))
            e.tensor_tensor(kind[:, b, :, :], over(k.col[:, 0:R], n), ps.recs[:, b, :, TYP:TYP + 1].to_broadcast([P, n, R]), ALU.is_equal)
            e.tensor_tensor(hot[:, b, :, :], over(k.col[:, :], n), ps.recs[:, b, :, LOC:LOC + 1].to_broadcast([P, n, P]), ALU.is_equal
                            ).then_inc(k.pass_sem["block"], 1)

        def count(e, g):
            if g.j % RG == 0:
                at[:] = windows_of(e, win, g, RG * GT)
            until(e, g.count(k.pass_sem["block"], 1, RG, 1 + CREDIT))
            b, first = g.j // RG % NREC, g.j % RG * GT
            for t in range(GT):
                m = e.matmul(totals[:, bass.ds(at[first + t], 1), :].rearrange("p a r -> p (a r)"), hot[:, b, first + t, :],
                             kind[:, b, first + t, :], start=False, stop=True, skip_group_check=True)
            m.then_inc(k.pass_sem["count"], 1)

        ps.stage("vector", "block", 1, LEAD, mark)
        ps.stage("tensor", "count", 1, 0, count)
        ps.run(None, 0, None, "count")


def totals_of(k):
    assert 512 % R == 0 and (W + 1) * R <= 1024
    return k.banks[:, 0:2, :].rearrange("p b n -> p (b n)")[:, 0:(W + 1) * R].rearrange("p (w r) -> p w r", r=R)


def count_edges(k):
    with ExitStack() as ctx:
        zero = scratch(k, ctx)("zero", [P, 512], BF16)
        t = k.dve.do(lambda e: e.memset(zero[:, :], 0.0))
        for i in range(2):
            k.pe.do(lambda e, i=i: e.matmul(k.psum[i][:, :], zero[:, 0:P], zero[:, :], start=True, stop=True), t)
        run_lanes(k)
    count_pass(k, k.rec_src, CS, k.win_src)
    k.dve.do(lambda e: e.tensor_tensor(k.inverse[:, 0:W, :], totals_of(k)[:, 0:W, :], k.sums[:, 0:W, H * (D + 1):], ALU.add))
    run_lanes(k)


def windows_of(e, win, g, n=GT):
    return e.bass.values_load_multi_w_load_instructions(win[0:1, bass.ds(g.tile(0), n)], engines=[e.engine],
                                                        min_val=0, max_val=W, skip_runtime_bounds_check_because=
                                                        "each is a sum of W comparisons, each 0 or 1")[1]


def sum_pass(k, rec, cols, win, table, acc, extra):
    n_all = F + extra
    with ExitStack() as ctx:
        sb = scratch(k, ctx)
        ps = Pass(k, rec, cols, win, IDX, LEAD)
        ps.recs = sb("recs", [P, NREC, RG * GT, cols])
        ps.far = sb("far", [P, RING, GT, F])
        hot = sb("hot", [P, RING, GT, P])

        def bank(g, t):
            at = t % 2 * n_all
            return k.psum[g.j % 4 * 2 + t // 2][:, at:at + n_all]

        def mark(e, g):
            until(e, ps.record(g))
            e.tensor_tensor(hot[:, g.j % RING, :, :], over(k.col[:, :], GT), ps.rows(g, LOC, LOC + 1).to_broadcast([P, GT, P]),
                            ALU.is_equal).then_inc(k.pass_sem["mark"], 1)

        def product(e, g):
            until(e, ps.at("mark", g))
            until(e, ps.gathered(g))
            until(e, ps.at_before("sum", g, 4))
            b = g.j % RING
            for t in range(GT):
                e.matmul(bank(g, t)[:, 0:F], hot[:, b, t, :], ps.far[:, b, t, :], start=True, stop=True)
                m = e.matmul(bank(g, t)[:, F:n_all], hot[:, b, t, :], ps.rows(g, ONE, ONE + extra)[:, t, :], start=True, stop=True)
            m.then_inc(k.pass_sem["product"], 1)

        def gather_up(e, g):
            at = windows_of(e, win, g)
            until(e, ps.at("product", g))
            for t in range(GT):
                w = at[t]
                until(e, ps.at("sum", g, t))
                e.tensor_tensor(acc[:, bass.ds(w, 1), :], bank(g, t).unsqueeze(1), acc[:, bass.ds(w, 1), :],
                                ALU.add).then_inc(k.pass_sem["sum"], 1)

        ps.stage("vector", "mark", 1, 3, mark)
        ps.stage("tensor", "product", 1, 1, product)
        ps.stage("vector", "sum", GT, 0, gather_up)
        ps.run(table, 1, "product", "sum")


def relation_pass(k, rec, cols, win, table, acc):
    with ExitStack() as ctx:
        sb = scratch(k, ctx)
        ps = Pass(k, rec, cols, win, IDX8, LEAD)
        ps.recs = sb("recs", [P, NREC, RG * GT, cols])
        ps.far = sb("far", [P, RING, GT, F])
        hot = sb("hot", [P, 4, GT, P], BF16)
        kind = sb("kind", [P, 4, GT, R])
        hot_t = sb("hot_t", [P, 4, GT, P])
        part = sb("part", [P, 2, GT, R])
        share = sb("share", [P, 2, GT])
        hot_s = sb("hot_s", [P, 4, GT, P])
        turned = [k.psum[i][:, 0:256].bitcast(BF16).rearrange("p (t n) -> p t n", t=GT) for i in (0, 1)]
        shares = [k.psum[i][:, 0:GT * R].rearrange("p (t r) -> p t r", t=GT) for i in (2, 3)]
        sums = [k.psum[i][:, :].rearrange("p (t f) -> p t f", t=GT) for i in (4, 5, 6, 7)]

        def mark(e, g):
            until(e, ps.record(g))
            b = g.j % 4
            e.tensor_tensor(kind[:, b, :, :], over(k.col[:, 0:R], GT), ps.rows(g, TYP, TYP + 1).to_broadcast([P, GT, R]), ALU.is_equal)
            e.tensor_tensor(hot[:, b, :, :], over(k.col[:, :], GT), ps.rows(g, LOC, LOC + 1).to_broadcast([P, GT, P]), ALU.is_equal
                            ).then_inc(k.pass_sem["mark"], 1)

        def turn(e, g):
            until(e, ps.at("mark", g))
            until(e, ps.at_before("flat", g, 2))
            for t in range(GT):
                m = e.transpose(turned[g.j % 2][:, t, :], hot[:, g.j % 4, t, :], k.ident_b[:, :])
            m.then_inc(k.pass_sem["turn"], 1)

        def flat(e, g):
            until(e, ps.at("turn", g))
            e.copy(hot_t[:, g.j % 4, :, :], turned[g.j % 2]).then_inc(k.pass_sem["flat"], 1)

        def look_up(e, g):
            at = windows_of(e, win, g)
            until(e, ps.at("flat", g))
            until(e, ps.at_before("weigh", g, 2, 1))
            for t in range(GT):
                w = at[t]
                m = e.matmul(shares[g.j % 2][:, t, :], hot_t[:, g.j % 4, t, :], k.inverse[:, bass.ds(w, 1), :].rearrange("p a r -> p (a r)"),
                             start=True, stop=True)
            m.then_inc(k.pass_sem["look"], 1)

        def weigh(e, g):
            b, b4 = g.j % 2, g.j % 4
            until(e, ps.at("look", g))
            e.tensor_tensor(part[:, b, :, :], shares[b], kind[:, b4, :, :], ALU.mult).then_inc(k.pass_sem["weigh"], 1)
            until(e, ps.at("weigh", g, 1))
            e.tensor_reduce(share[:, b, :], part[:, b, :, :], AX, ALU.add).then_inc(k.pass_sem["weigh"], 1)
            until(e, ps.at("weigh", g, 2))
            e.tensor_tensor(hot_s[:, b4, :, :], hot[:, b4, :, :], wide(share[:, b, :], P), ALU.mult).then_inc(k.pass_sem["weigh"], 1)

        def product(e, g):
            until(e, ps.at("weigh", g))
            until(e, ps.gathered(g))
            until(e, ps.at_before("sum", g, 4))
            for t in range(GT):
                m = e.matmul(sums[g.j % 4][:, t, :], hot_s[:, g.j % 4, t, :], ps.far[:, g.j % RING, t, :], start=True, stop=True)
            m.then_inc(k.pass_sem["product"], 1)

        def gather_up(e, g):
            at = windows_of(e, win, g)
            until(e, ps.at("product", g))
            for t in range(GT):
                w = at[t]
                until(e, ps.at("sum", g, t))
                e.tensor_tensor(acc[:, bass.ds(w, 1), :], sums[g.j % 4][:, t:t + 1, :], acc[:, bass.ds(w, 1), :],
                                ALU.add).then_inc(k.pass_sem["sum"], 1)

        ps.stage("vector", "mark", 1, 3, mark)
        ps.stage("vector", "weigh", 3, 1, weigh)
        ps.stage("scalar", "flat", 1, 3, flat)
        ps.stage("tensor", "product", 1, 0, product)
        ps.stage("tensor", "look", 1, 2, look_up)
        ps.stage("tensor", "turn", 1, 3, turn)
        ps.stage("vector", "sum", GT, 0, gather_up)
        ps.run(table, 0, "product", "sum")


def attention_pass(k, rec, cols, win, table, keys, top, acc):
    D1 = D + 1
    HD = H * D1
    with ExitStack() as ctx:
        sb = scratch(k, ctx)
        ps = Pass(k, rec, cols, win, IDX, 5)
        ps.recs = sb("recs", [P, NREC, RG * GT, cols])
        ps.far = sb("far", [P, RING, GT, 2 * F])
        hot = sb("hot", [P, 8, GT, P], BF16)
        hot_f = sb("hot_f", [P, 2, GT, P])
        cold = sb("cold", [P, 2, GT, P], BF16)
        hot_t = sb("hot_t", [P, 4, GT, P])
        qk = sb("qk", [P, 1, GT, F])
        score = sb("score", [P, 4, GT * H])
        s_hi = sb("s_hi", [P, 2, GT * H], BF16)
        s_lo = sb("s_lo", [P, 2, GT * H], BF16)
        tile_top = sb("tile_top", [P, 2, GT, H])
        old_top = sb("old_top", [P, 2, GT, H])
        tops_at, sums_at = {}, {}
        new_top = sb("new_top", [P, 2, GT, H])
        drop = sb("drop", [P, 4, GT, H])
        over_top = sb("over_top", [P, 2, GT * H])
        mix = sb("mix", [P, 2, GT, HD + R])
        mixed = [mix[:, b, :, 0:HD].rearrange("p t (h d) -> p t h d", h=H) for b in (0, 1)]
        away = sb("away", [P, GT, P], BF16)
        sums = [k.psum[t // 2][:, t % 2 * (HD + R):(t % 2 + 1) * (HD + R)] for t in range(GT)]
        key_rows = k.psum[2][:, :].rearrange("p (t f) -> p t f", t=GT)
        turned = k.psum[3][:, 0:256].bitcast(BF16).rearrange("p (t n) -> p t n", t=GT)
        top_rows = k.psum[3][:, 256:256 + GT * H]
        spread = k.banks[:, 4:4 + GT, :]

        def score_products(e, g):
            until(e, ps.at("key", g))
            until(e, ps.gathered(g))
            e.tensor_tensor(qk[:, 0, :, :], ps.far[:, g.j % RING, :, 0:F], key_rows, ALU.mult).then_inc(k.pass_sem["score"], 1)

        def score_sums(e, g):
            until(e, ps.at("score", g, 1))
            e.tensor_reduce(score[:, g.j % 4, :], qk[:, 0, :, :].rearrange("p t (h d) -> p (t h) d", h=H), AX, ALU.add
                            ).then_inc(k.pass_sem["score"], 1)

        def score_high(e, g):
            until(e, ps.at("score", g, 2))
            until(e, ps.at_before("spread", g, 2))
            e.tensor_copy(s_hi[:, g.j % 2, :], score[:, g.j % 4, :]).then_inc(k.pass_sem["score"], 1)

        def score_low(e, g):
            until(e, ps.at("score", g, 3))
            e.tensor_tensor(s_lo[:, g.j % 2, :], score[:, g.j % 4, :], s_hi[:, g.j % 2, :], ALU.subtract
                            ).then_inc(k.pass_sem["score"], 1)

        def tile_tops(half):
            def work(e, g):
                until(e, ps.at("spread", g, half + 1))
                t = 2 * half
                e.tensor_reduce(tile_top[:, g.j % 2, t:t + 2, :].rearrange("p t h -> p (t h)"),
                                spread[:, t:t + 2, :].rearrange("p t (h n) -> p (t h) n", h=H), AX, ALU.max
                                ).then_inc(k.pass_sem["reduce"], 1)
            return work

        def running_top(t):
            def work(e, g):
                if t == 0:
                    tops_at[g.j] = windows_of(e, win, g)
                    until(e, ps.at("reduce", g))
                    until(e, ps.at_before("fade", g, 2))
                mine = top[:, bass.ds(tops_at[g.j][t], 1), :].rearrange("p a h -> p (a h)")
                until(e, ps.at("top", g, t))
                e.tensor_tensor(old_top[:, g.j % 2, t, :], mine, mine, ALU.max)
                e.tensor_tensor(mine, mine, tile_top[:, g.j % 2, t, :], ALU.max).then_inc(k.pass_sem["top"], 1)
            return work

        def new_tops(e, g):
            b = g.j % 2
            until(e, ps.at("top", g, GT))
            e.tensor_tensor(new_top[:, b, :, :], old_top[:, b, :, :], tile_top[:, b, :, :], ALU.max).then_inc(k.pass_sem["top"], 1)

        def drops(e, g):
            b = g.j % 2
            until(e, ps.at("top", g, GT + 1))
            e.tensor_tensor(drop[:, g.j % 4, :, :], old_top[:, b, :, :], new_top[:, b, :, :], ALU.subtract).then_inc(k.pass_sem["top"], 1)

        def below(e, g):
            until(e, ps.at("top_row", g))
            until(e, ps.at("score", g))
            e.tensor_tensor(over_top[:, g.j % 2, :], score[:, g.j % 4, :], top_rows, ALU.subtract).then_inc(k.pass_sem["below"], 1)

        def mixes(e, g):
            b = g.j % 2
            until(e, ps.at_before("product", g, 2))
            e.tensor_tensor(mix[:, b, :, HD:], over(k.col[:, 0:R], GT), ps.rows(g, TYP, TYP + 1).to_broadcast([P, GT, R]), ALU.is_equal)
            until(e, ps.at("weight", g))
            e.tensor_tensor(mixed[b][:, :, :, 0:D], ps.far[:, g.j % RING, :, F:2 * F].rearrange("p t (h d) -> p t h d", h=H),
                            mixed[b][:, :, :, D:D1].to_broadcast([P, GT, H, D]), ALU.mult).then_inc(k.pass_sem["mix"], 1)

        def fade_sum(t):
            def work(e, g):
                if t == 0:
                    sums_at[g.j] = windows_of(e, win, g)
                    until(e, ps.at("fade", g))
                mine = acc[:, bass.ds(sums_at[g.j][t], 1), 0:HD].rearrange("p a (h d) -> p (a h) d", h=H)
                until(e, ps.at("sum", g, 2 * t))
                e.tensor_tensor(mine, mine, wide(drop[:, g.j % 4, t, :], D1), ALU.mult).then_inc(k.pass_sem["sum"], 1)
            return work

        def gather_up(t):
            def work(e, g):
                if t == 0:
                    until(e, ps.at("product", g))
                mine = acc[:, bass.ds(sums_at[g.j][t], 1), :].rearrange("p a c -> p (a c)")
                until(e, ps.at("sum", g, 2 * t + 1))
                e.tensor_tensor(mine, mine, sums[t], ALU.add).then_inc(k.pass_sem["sum"], 1)
            return work

        def weights(e, g):
            until(e, ps.at("below", g))
            until(e, ps.at_before("product", g, 2))
            e.activation(mixed[g.j % 2][:, :, :, D], over_top[:, g.j % 2, :].rearrange("p (t h) -> p t h", t=GT), ACT.Exp).then_inc(k.pass_sem["weight"], 1)

        def distance(e, g):
            until(e, ps.record(g))
            until(e, ps.at_before("mark", g, 1))
            for t in range(GT):
                m = e.activation(away[:, t, :], k.col[:, :], ACT.Abs, bias=ps.rows(g, LOC, LOC + 1)[:, t, :], scale=-1.0)
            m.then_inc(k.pass_sem["mark"], 1)

        def mark(e, g):
            until(e, ps.at("mark", g, 1))
            until(e, ps.at_before("product", g, 8))
            e.activation(hot[:, g.j % 8, :, :], away[:, :, :], ACT.Relu, bias=k.ones[:, 0:1], scale=-1.0).then_inc(k.pass_sem["mark"], 1)

        def flat(e, g):
            until(e, ps.at("turn", g))
            until(e, ps.at_before("top_row", g, 4))
            e.copy(hot_t[:, g.j % 4, :, :], turned).then_inc(k.pass_sem["flat"], 1)

        def chill(e, g):
            until(e, ps.at("mark", g))
            until(e, ps.at_before("spread", g, 2))
            e.activation(cold[:, g.j % 2, :, :], hot[:, g.j % 8, :, :], ACT.Copy, bias=1.0, scale=-1.0).then_inc(k.pass_sem["chill"], 1)

        def widen(e, g):
            until(e, ps.at("mark", g))
            until(e, ps.at_before("product", g, 2))
            e.copy(hot_f[:, g.j % 2, :, :], hot[:, g.j % 8, :, :]).then_inc(k.pass_sem["widen"], 1)

        def fade(e, g):
            until(e, ps.at("top", g))
            e.activation(drop[:, g.j % 4, :, :], drop[:, g.j % 4, :, :], ACT.Exp).then_inc(k.pass_sem["fade"], 1)

        def keys_of(e, g):
            at = windows_of(e, win, g)
            until(e, ps.at("flat", g))
            until(e, ps.at_before("score", g, 1, 1))
            for t in range(GT):
                w = at[t]
                m = e.matmul(key_rows[:, t, :], hot_t[:, g.j % 4, t, :], keys[:, bass.ds(w, 1), :].rearrange("p a f -> p (a f)"),
                             start=True, stop=True)
            m.then_inc(k.pass_sem["key"], 1)

        def turn(e, g):
            until(e, ps.at("mark", g))
            until(e, ps.at_before("below", g, 4))
            until(e, ps.at_before("flat", g, 1))
            for t in range(GT):
                m = e.transpose(turned[:, t, :], hot[:, g.j % 8, t, :], k.ident_b[:, :])
            m.then_inc(k.pass_sem["turn"], 1)

        def top_row(e, g):
            until(e, ps.at("top", g, GT + 1))
            until(e, ps.at_before("flat", g, -3))
            until(e, ps.at_before("below", g, 1))
            for t in range(GT):
                m = e.matmul(top_rows[:, t * H:(t + 1) * H], hot_t[:, g.j % 4, t, :], new_top[:, g.j % 2, t, :], start=True, stop=True)
            m.then_inc(k.pass_sem["top_row"], 1)

        def product(e, g):
            until(e, ps.at("mix", g))
            until(e, ps.at("widen", g))
            until(e, ps.at_before("sum", g, 1))
            for t in range(GT):
                m = e.matmul(sums[t], hot_f[:, g.j % 2, t, :], mix[:, g.j % 2, t, :], start=True, stop=True)
            m.then_inc(k.pass_sem["product"], 1)

        def spreads(half):
            def work(e, g):
                b = g.j % 2
                if half == 0:
                    until(e, ps.at("score", g))
                    until(e, ps.at("chill", g))
                until(e, ps.at_before("reduce", g, 1, half + 1))
                for t in (2 * half, 2 * half + 1):
                    e.matmul(spread[:, t, :], cold[:, b, t, :], k.none4[:, :, :].rearrange("p h n -> p (h n)"),
                             start=True, stop=False, skip_group_check=True)
                    for h in range(H):
                        c = t * H + h
                        for s in (s_hi, s_lo):
                            m = e.matmul(spread[:, t, h * P:(h + 1) * P], s[:, b, c:c + 1].to_broadcast([P, P]), k.ident_b[:, :],
                                         start=False, stop=(h == H - 1 and s is s_lo), skip_group_check=True)
                m.then_inc(k.pass_sem["spread"], 1)
            return work

        ps.stage("vector", "top", GT + 2, 1, running_top(0))
        ps.stage("vector", "sum", 2 * GT, 0, fade_sum(0))
        ps.stage("vector", "top", GT + 2, 1, running_top(1))
        ps.stage("vector", "score", 4, 3, score_sums)
        ps.stage("vector", "top", GT + 2, 1, running_top(2))
        ps.stage("vector", "sum", 2 * GT, 0, gather_up(0))
        ps.stage("vector", "top", GT + 2, 1, running_top(3))
        ps.stage("vector", "sum", 2 * GT, 0, fade_sum(1))
        ps.stage("vector", "top", GT + 2, 1, new_tops)
        ps.stage("vector", "score", 4, 3, score_high)
        ps.stage("vector", "sum", 2 * GT, 0, gather_up(1))
        ps.stage("vector", "top", GT + 2, 1, drops)
        ps.stage("vector", "score", 4, 3, score_low)
        ps.stage("vector", "sum", 2 * GT, 0, fade_sum(2))
        ps.stage("vector", "below", 1, 1, below)
        ps.stage("vector", "sum", 2 * GT, 0, gather_up(2))
        ps.stage("vector", "reduce", 2, 2, tile_tops(0))
        ps.stage("vector", "sum", 2 * GT, 0, fade_sum(3))
        ps.stage("vector", "mix", 1, 1, mixes)
        ps.stage("vector", "sum", 2 * GT, 0, gather_up(3))
        ps.stage("vector", "reduce", 2, 2, tile_tops(1))
        ps.stage("vector", "score", 4, 4, score_products)
        ps.stage("scalar", "mark", 2, 5, distance)
        ps.stage("scalar", "chill", 1, 3, chill)
        ps.stage("scalar", "mark", 2, 5, mark)
        ps.stage("scalar", "widen", 1, 1, widen)
        ps.stage("scalar", "weight", 1, 1, weights)
        ps.stage("scalar", "fade", 1, 1, fade)
        ps.stage("scalar", "flat", 1, 5, flat)
        ps.stage("tensor", "key", 1, 4, keys_of)
        ps.stage("tensor", "spread", 2, 2, spreads(0))
        ps.stage("tensor", "top_row", 1, 1, top_row)
        ps.stage("tensor", "spread", 2, 2, spreads(1))
        ps.stage("tensor", "turn", 1, 5, turn)
        ps.stage("tensor", "product", 1, 1, product)
        ps.run(table, 4, "mix", "sum", SourceRecords(k, sb))



def root(k, variance, ready):
    t = k.dve.do(lambda e: e.tensor_scalar(variance, variance, EPS, None, ALU.add), ready)
    t = k.act.do(lambda e: e.activation(variance, variance, ACT.Sqrt), t)
    return k.dve.do(lambda e: e.reciprocal(variance, variance), t)


def normalize(k, x, stats, moments, n, ready):
    dve = k.dve
    for i in range(n):
        t = dve.do(lambda e, i=i: e.bn_stats(stats[:, i, :], x[:, i, :]), *ready)
    for i in range(n):
        t = dve.do(lambda e, i=i: e.bn_aggr(moments[:, i, :], stats[:, i, :]), t)
    t = root(k, moments[:, 0:n, 1], t)
    return dve.do(lambda e: e.scalar_tensor_tensor(out=moments[:, 0:n, 0], in0=moments[:, 0:n, 0], scalar=-1.0,
                                                   in1=moments[:, 0:n, 1], op0=ALU.mult, op1=ALU.mult), t)


def load_rows(k, pairs):
    for to, of in pairs:
        t = k.sp.dma(lambda e, to=to, of=of: e.dma_start(to, of), k.load)
    return t


def turn_window(k, source, bank, to, ready, bank_free, to_free):
    t = k.pe.do(lambda e: e.transpose(bank[:, 0:P], source, k.ident[:, :]), *ready, *bank_free)
    return k.act.do(lambda e: e.copy(to, bank[:, 0:P]), t, *to_free)


C7 = 7
assert W % C7 == 0


def attention_tables(k, sb):
    dve, act, pe, sp, a = k.dve, k.act, k.pe, k.sp, k.a
    w4 = sb("w4", [P, 4, F])
    b4 = sb("b4", [1, 4, F])
    xin = sb("xin", [P, 2, C7, F])
    stats = sb("stats", [P, 2, C7, 6])
    moments = sb("moments", [P, 2, C7, 2])
    h = sb("h", [P, 2, F])
    ht = sb("ht", [P, 2, F])
    qv = sb("qv", [P, 4, 2 * F])
    kept = sb("kept", [P, 4, 2 * F])
    names = ("q", "v", "k", "s")
    t_w = load_rows(k, [(w4[:, i, :], a[f"L0_gnn_W{c}"]) for i, c in enumerate(names)]
                    + [(b4[:, i, :], a[f"L0_gnn_b{c}"].rearrange("(a f) -> a f", a=1)) for i, c in enumerate(names)])
    x_rows = a["x"].rearrange("(w p) f -> p w f", p=P)
    qv_rows = k.table_qv.rearrange("(w p) f -> w p f", p=P)
    yield
    t_x, t_h, t_ht, t_pe = [None] * (W // C7), {}, {}, {}
    t_norm, t_q, t_v = {}, {}, {}
    got = lambda d, i: [d[i]] if i in d else []

    def fetch(c):
        t_x[c] = sp.dma(lambda e: e.dma_start(xin[:, c % 2, :, :], x_rows[:, c * C7:(c + 1) * C7, :]),
                        k.x_in[c % 2], *got(t_h, (c - 1) * C7 - 1))
    fetch(0)
    for c in range(W // C7):
        if c + 1 < W // C7:
            fetch(c + 1)
        t_norm[c] = normalize(k, xin[:, c % 2, :, :], stats[:, c % 2, :, :], moments[:, c % 2, :, :], C7,
                              [t_x[c], *got(t_h, (c - 1) * C7 - 1)])
        for i in range(C7):
            w = c * C7 + i
            b, s = w % 2, w % 4
            t_h[w] = act.do(lambda e, c=c, i=i, b=b: e.activation(
                h[:, b, :], xin[:, c % 2, i, :], ACT.Relu, bias=moments[:, c % 2, i, 0:1], scale=moments[:, c % 2, i, 1:2]),
                t_norm[c], *got(t_ht, w - 2))
            t_ht[w] = turn_window(k, h[:, b, :], k.psum[b], ht[:, b, :], [t_h[w]], got(t_ht, w - 2), got(t_pe, w - 2))
            bank = k.psum[2 + s]
            pe.do(lambda e, b=b, bank=bank: e.matmul(bank[:, :], ht[:, b, :], w4[:, :, :].rearrange("p a f -> p (a f)"), start=True, stop=False),
                  t_ht[w], t_w, *got(t_q, w - 4), *got(t_v, w - 4))
            t_pe[w] = pe.do(lambda e, bank=bank: e.matmul(bank[:, :], k.ones[0:1, :], b4[:, :, :].rearrange("p a f -> p (a f)"), start=False, stop=True))
            t_v[w] = dve.do(lambda e, s=s, bank=bank: e.tensor_copy(qv[:, s, :], bank[:, 0:2 * F]), t_pe[w], *got(k.t_qv, w - 4))
            act.do(lambda e, s=s, bank=bank: e.activation(kept[:, s, 0:F], bank[:, 2 * F:3 * F], ACT.Copy, scale=float(D) ** -0.5), t_v[w], *got(k.t_kept, w - 4))
            t_q[w] = act.do(lambda e, s=s, bank=bank: e.copy(kept[:, s, F:2 * F], bank[:, 3 * F:4 * F]))
            k.t_qv[w] = sp.dma(lambda e, w=w, s=s: e.dma_start(qv_rows[w], qv[:, s, :]), k.qv_out[s], t_v[w])
            k.t_kept[w] = sp.dma(lambda e, w=w, s=s: e.dma_start(k.kept[:, w, :], kept[:, s, :]), k.kept_out[s], t_q[w])
            yield
    for s in range(4):
        sp.wait(k.qv_out[s].token, k.kept_out[s].token)
    yield


def attention_end(k, sb):
    dve, act, sp, a = k.dve, k.act, k.sp, k.a
    wg = sb("wg", [P, 3, F])
    w_skip, w_agg = sb("w_skip", [P, F]), sb("w_agg", [P, F])
    bg, alpha = sb("bg", [P, 1]), sb("alpha", [P, 1])
    gamma, beta = sb("gamma", [P, F]), sb("beta", [P, F])
    skip = sb("skip", [P, 2, C7, F])
    agg = sb("agg", [P, C7, F])
    tmp = sb("tmp", [P, C7, F])
    tmp2 = sb("tmp2", [P, C7, F])
    den = sb("den", [P, C7, H])
    z = sb("z", [P, 2, C7])
    stats = sb("stats", [P, C7, 6])
    moments = sb("moments", [P, C7, 2])
    every = lambda name, n: a[name].rearrange("(a n) -> a n", a=1).to_broadcast([P, n])
    x_rows = a["x"].rearrange("(w p) f -> p w f", p=P)
    load_rows(k, [(k.x[:, 0:W, :], x_rows),
                  (wg[:, :, :].rearrange("p a f -> p (a f)"), a["L0_gnn_Wg"].rearrange("n a -> a n").to_broadcast([P, 3 * F])),
                  (bg[:, :], every("L0_gnn_bg", 1)), (alpha[:, :], every("L0_gnn_alpha", 1)),
                  (gamma[:, :], every("L0_gnn_gamma", F))])
    load_rows(k, [(beta[:, :], every("L0_gnn_beta", F))])
    yield
    t_w = k.load.token
    dve.do(lambda e: e.tensor_tensor(w_skip[:, :], wg[:, 0, :], wg[:, 2, :], ALU.add), t_w)
    t = dve.do(lambda e: e.tensor_tensor(w_agg[:, :], wg[:, 1, :], wg[:, 2, :], ALU.subtract))
    sums = k.sums[:, :, 0:H * (D + 1)].rearrange("p w (h d) -> p w h d", h=H)
    t_s, t_use = {}, {}

    def fetch(c):
        t_s[c] = sp.dma(lambda e: e.dma_start(skip[:, c % 2, :, :], k.kept[:, c * C7:(c + 1) * C7, F:2 * F]), k.x_in[c % 2],
                        *([t_use[c - 2]] if c >= 2 else []))
    fetch(0)
    fetch(1)
    for c in range(W // C7):
        b = c % 2
        s = skip[:, b, :, :]
        mine = sums[:, c * C7:(c + 1) * C7, :, :]
        x = k.x[:, c * C7:(c + 1) * C7, :]
        t = dve.do(lambda e, m=mine: e.tensor_scalar(den[:, :, :], m[:, :, :, D], 0.0, None, ALU.is_equal), t)
        t = dve.do(lambda e, m=mine: e.tensor_tensor(den[:, :, :], den[:, :, :], m[:, :, :, D], ALU.add), t)
        t = dve.do(lambda e: e.reciprocal(den[:, :, :], den[:, :, :]), t)
        t = dve.do(lambda e, m=mine: e.tensor_tensor(agg[:, :, :].rearrange("p w (h d) -> p w h d", h=H), m[:, :, :, 0:D],
                                                      den[:, :, :].unsqueeze(3).to_broadcast([P, C7, H, D]), ALU.mult), t)
        yield
        t = dve.do(lambda e: e.tensor_tensor(tmp[:, :, :], agg[:, :, :], over(w_agg[:, :], C7), ALU.mult), t)
        t2 = dve.do(lambda e, s=s: e.tensor_tensor(tmp2[:, :, :], s, over(w_skip[:, :], C7), ALU.mult), t_s[c])
        t = dve.do(lambda e: e.tensor_tensor(tmp[:, :, :], tmp[:, :, :], tmp2[:, :, :], ALU.add), t, t2)
        t = dve.do(lambda e, b=b: e.tensor_reduce(z[:, b, :], tmp[:, :, :], AX, ALU.add), t)
        t_g = act.do(lambda e, b=b: e.activation(z[:, b, :], z[:, b, :], ACT.Sigmoid, bias=bg[:, :]), t, t_w)
        yield
        t = dve.do(lambda e, s=s: e.tensor_tensor(tmp[:, :, :], s, agg[:, :, :], ALU.subtract), t)
        t_use[c] = t
        if c + 2 < W // C7:
            fetch(c + 2)
        t = dve.do(lambda e, b=b: e.tensor_tensor(tmp[:, :, :], tmp[:, :, :], wide(z[:, b, :], F), ALU.mult), t, t_g)
        yield
        t = dve.do(lambda e: e.tensor_tensor(agg[:, :, :], agg[:, :, :], tmp[:, :, :], ALU.add), t)
        t = normalize(k, agg[:, :, :], stats[:, :, :], moments[:, :, :], C7, [t])
        yield
        t = dve.do(lambda e: e.tensor_tensor(tmp[:, :, :], agg[:, :, :], wide(moments[:, :, 1], F), ALU.mult), t)
        t = dve.do(lambda e: e.tensor_tensor(tmp[:, :, :], tmp[:, :, :], wide(moments[:, :, 0], F), ALU.add), t)
        yield
        t = dve.do(lambda e: e.tensor_tensor(tmp[:, :, :], tmp[:, :, :], over(gamma[:, :], C7), ALU.mult), t)
        t = dve.do(lambda e: e.tensor_tensor(tmp[:, :, :], tmp[:, :, :], over(beta[:, :], C7), ALU.add), t)
        t = dve.do(lambda e: e.tensor_scalar(tmp2[:, :, :], tmp[:, :, :], 0.0, alpha[:, 0:1], ALU.min, ALU.mult), t)
        yield
        t = dve.do(lambda e: e.scalar_tensor_tensor(out=tmp[:, :, :], in0=tmp[:, :, :], scalar=0.0, in1=tmp2[:, :, :],
                                                    op0=ALU.max, op1=ALU.add), t)
        t = dve.do(lambda e, x=x: e.tensor_tensor(x, x, tmp[:, :, :], ALU.add), t)
        yield


def relation_tables(k, sb, before):
    dve, act, pe, sp, a = k.dve, k.act, k.pe, k.sp, k.a
    wr = sb("wr", [P, R, F])
    ws = sb("ws", [P, F])
    stats = sb("stats", [P, C7, 6])
    moments = sb("moments", [P, 2, C7, 2])
    seen = sb("seen", [P, W, R])
    h = sb("h", [P, 2, F])
    ht = sb("ht", [P, 2, F])
    xw = sb("xw", [P, 4, R * F])
    load_rows(k, [(wr[:, :, :], a["L1_gnn_weight"].rearrange("r i o -> i r o"))])
    load_rows(k, [(ws[:, :], a["L1_gnn_self_weight"])])
    next(before)
    t_w = k.load.token
    for _ in range(C7 + 2):
        next(before)
    cnt = k.inverse[:, 0:W, :]
    t = dve.do(lambda e: e.tensor_scalar(seen[:, :, :], cnt, 0.0, None, ALU.is_gt))
    t = dve.do(lambda e: e.tensor_scalar(cnt, cnt, 1.0, None, ALU.max), t)
    t = dve.do(lambda e: e.reciprocal(cnt, cnt), t)
    dve.do(lambda e: e.tensor_tensor(cnt, cnt, seen[:, :, :], ALU.mult), t)
    dve.do(lambda e: e.memset(k.inverse[:, W, :], 0.0))
    xw_rows = k.table_xw.rearrange("(w p r) f -> w p (r f)", p=P, r=R)
    t_h, t_ht, t_pe, t_a, t_b, t_c, t_out = ({} for _ in range(7))
    got = lambda d, i: [d[i]] if i in d else []

    def rows_of(w):
        (c, i), b = divmod(w, C7), w % 2
        x = k.x[:, c * C7:(c + 1) * C7, :]
        if i == 0:
            t_n[c] = normalize(k, x, stats[:, :, :], moments[:, c % 2, :, :], C7, [(dve.sem, dve.n), *got(t_h, (c - 1) * C7 - 1)])
        t_h[w] = act.do(lambda e: e.activation(h[:, b, :], x[:, i, :], ACT.Relu, bias=moments[:, c % 2, i, 0:1],
                                               scale=moments[:, c % 2, i, 1:2]), t_n[c], *got(t_ht, w - 2))

    def turned(w):
        b = w % 2
        t_ht[w] = turn_window(k, h[:, b, :], k.psum[b], ht[:, b, :], [t_h[w]], got(t_ht, w - 2), got(t_pe, w - 2))

    t_n = {}
    rows_of(0)
    turned(0)
    rows_of(1)
    for w in range(W):
        b, s = w % 2, w % 4
        if w + 2 < W:
            rows_of(w + 2)
        if w + 1 < W:
            turned(w + 1)
        lo, hi, own = k.psum[2 + b], k.psum[4 + b], k.psum[6 + b]
        pe.do(lambda e, b=b, lo=lo: e.matmul(lo[:, :], ht[:, b, :], wr[:, 0:4, :].rearrange("p r f -> p (r f)"), start=True, stop=True),
              t_ht[w], t_w, *got(t_a, w - 2))
        pe.do(lambda e, b=b, hi=hi: e.matmul(hi[:, :], ht[:, b, :], wr[:, 4:8, :].rearrange("p r f -> p (r f)"), start=True, stop=True),
              *got(t_b, w - 2))
        t_pe[w] = pe.do(lambda e, b=b, own=own: e.matmul(own[:, 0:F], ht[:, b, :], ws[:, :], start=True, stop=True), *got(t_c, w - 2))
        t_a[w] = dve.do(lambda e, s=s, lo=lo: e.tensor_copy(xw[:, s, 0:4 * F], lo[:, :]), t_pe[w], *got(t_out, w - 4))
        t_b[w] = act.do(lambda e, s=s, hi=hi: e.copy(xw[:, s, 4 * F:8 * F], hi[:, :]), t_pe[w], *got(t_out, w - 4))
        t_c[w] = dve.do(lambda e, w=w, own=own: e.tensor_copy(k.acc[:, w, :], own[:, 0:F]))
        t_out[w] = sp.dma(lambda e, w=w, s=s: e.dma_start(xw_rows[w], xw[:, s, :]), k.qv_out[s], t_a[w], t_b[w])
        next(before, None)
    dve.do(lambda e: e.memset(k.acc[:, W, :], 0.0), (dve.sem, dve.n))
    for s in range(4):
        sp.wait(k.qv_out[s].token)


def attention_to_relation(k):
    with ExitStack() as ctx:
        relation_tables(k, scratch(k, ctx), attention_end(k, scratch(k, ctx)))
        run_lanes(k)


def plain_table(k, sb, w0, n, ready, state):
    act, sp = k.act, k.sp
    c = state["c"]
    state["c"] += 1
    b = c % 2
    x = k.x[:, w0:w0 + n, :]
    h, stats, moments = state["h"], state["stats"], state["moments"]
    t = normalize(k, x, stats[:, b, :, :], moments[:, b, :, :], n, [*ready, *state["done"].get(c - 2, [])])
    for i in range(n):
        t_h = act.do(lambda e, i=i: e.activation(h[:, b, i, :], x[:, i, :], ACT.Relu, bias=moments[:, b, i, 0:1],
                                                 scale=moments[:, b, i, 1:2]), t, *state["done"].get(c - 2, []), *state["used"].get(c - 2, []))
    rows = k.table_h.rearrange("(w p) f -> p w f", p=P)
    t_o = sp.dma(lambda e: e.dma_start(rows[:, w0:w0 + n, :], h[:, b, 0:n, :]), k.x_in[b], t_h)
    state["done"][c] = [t_o, t_h]
    return h[:, b, :, :], t_h, c


def table_state(k, sb, n):
    return {"c": 0, "done": {}, "used": {}, "h": sb("h", [P, 2, n, F]), "stats": sb("stats", [P, 2, n, 6]), "moments": sb("moments", [P, 2, n, 2])}


def gine_tables(k):
    dve, sp = k.dve, k.sp
    with ExitStack() as ctx:
        sb = scratch(k, ctx)
        state = table_state(k, sb, C7)
        for c in range(W // C7):
            t = dve.do(lambda e, c=c: e.tensor_tensor(k.x[:, c * C7:(c + 1) * C7, :], k.x[:, c * C7:(c + 1) * C7, :],
                                                      k.acc[:, c * C7:(c + 1) * C7, :], ALU.add))
        t = dve.do(lambda e: e.memset(k.acc17[:, :, F:F + 17], 0.0), t)
        dve.do(lambda e: e.memset(k.acc17[:, 0:W, F:F + 1], 1.0), t)
        dve.do(lambda e: e.memset(k.acc17[:, 0:W, F + 1:F + 2], 4.0))
        t = dve.do(lambda e: e.memset(k.acc17[:, W, 0:F], 0.0))
        for c in range(W // C7):
            h, t_h, n = plain_table(k, sb, c * C7, C7, [t], state)
            t_u = dve.do(lambda e, c=c, h=h: e.tensor_copy(k.acc17[:, c * C7:(c + 1) * C7, 0:F], h), t_h)
            state["used"][n] = [t_u]
        sp.wait(k.x_in[0].token, k.x_in[1].token)
        run_lanes(k)


G4 = 4
BLOCKS = [(w, min(G4, W - w)) for w in range(0, W, G4)]


def column(ap, n):
    return ap.rearrange("(c p) -> p c", p=n)


def gine_end(k):
    dve, act, pe, sp, pool, a = k.dve, k.act, k.pe, k.sp, k.pool, k.a
    got = lambda d, i: [d[i]] if i in d else []
    with ExitStack() as ctx:
        sb = scratch(k, ctx)
        wc = sb("wc", [17, F])
        w1 = sb("w1", [P, 2 * F])
        w2 = sb("w2", [P, 2, F])
        b2 = sb("b2", [1, F])
        cols = sb("cols", [P, 3, 2])
        et = sb("et", [17, 2, G4 * P])
        aggt = sb("aggt", [P, 2, G4 * P])
        hid = sb("hid", [P, 2, 2, G4 * P])
        stats = sb("bn_stats", [P, 2, len(BLOCKS), 6])
        moments = sb("bn_moments", [P, 2, 2])
        hot = sb("relu", [P, 2, 2, G4 * P])
        state = table_state(k, sb, G4)
        with k.nc.allow_non_contiguous_dma(reason="three vectors of 256"):
            load_rows(k, [(cols[:, i, :], column(a[f"L2_gnn_{n}"], P)) for i, n in enumerate(("b1", "gamma", "beta"))])
            t_w = load_rows(k, [(wc[0:1, :], a["L2_gnn_b_edge"].rearrange("(a n) -> a n", a=1)), (wc[1:17, :], a["L2_gnn_W_edge"]),
                                (w1[:, :], a["L2_gnn_W1"]), (w2[:, :, :], a["L2_gnn_W2"].rearrange("(c p) f -> p c f", p=P)),
                                (b2[:, :], a["L2_gnn_b2"].rearrange("(a n) -> a n", a=1))])
            run_lanes(k)
        t_e, t_agg, t_hp, t_ev, t_out, t_st = ({} for _ in range(6))
        for j, (w0, n) in enumerate(BLOCKS):
            b = j % 2
            pe_e, pe_a = k.psum[b], k.psum[2 + b]
            m = n * P
            for i in range(n):
                t = pe.do(lambda e, i=i, w0=w0, p=pe_e: e.transpose(p[0:17, i * P:(i + 1) * P], k.acc17[:, w0 + i, F:F + 17], k.ident[:, :]), *got(t_e, j - 2))
            t_e[j] = act.do(lambda e, b=b, m=m, p=pe_e: e.copy(et[:, b, 0:m], p[0:17, 0:m]), t, *got(t_agg, j - 2))
            for i in range(n):
                pe.do(lambda e, i=i, w0=w0, p=pe_a: e.matmul(p[:, i * P:(i + 1) * P], k.acc17[:, w0 + i, 0:F], k.ident[:, :], start=True, stop=False), *got(t_agg, j - 2))
                t = pe.do(lambda e, i=i, b=b, p=pe_a: e.matmul(p[:, i * P:(i + 1) * P], wc[:, :], et[:, b, i * P:(i + 1) * P], start=False, stop=True), t_e[j], t_w)
            t_agg[j] = dve.do(lambda e, b=b, m=m, p=pe_a: e.tensor_copy(aggt[:, b, 0:m], p[:, 0:m]), t, *got(t_hp, j - 2))
            for c in range(2):
                t_hp[j] = pe.do(lambda e, b=b, c=c, m=m: e.matmul(k.psum[4 + 2 * b + c][:, 0:m], w1[:, c * F:(c + 1) * F], aggt[:, b, 0:m], start=True, stop=True),
                                t_agg[j], *got(t_ev, j - 2))
            for c in range(2):
                t_ev[j] = act.do(lambda e, b=b, c=c, m=m: e.activation(hid[:, b, c, 0:m], k.psum[4 + 2 * b + c][:, 0:m], ACT.Identity, bias=cols[:, 0, c:c + 1]),
                                 t_hp[j], *got(t_out, j - 2), *got(t_st, j - 2))
            real = m if w0 + n < W else m - P + LAST
            for c in range(2):
                t_st[j] = dve.do(lambda e, j=j, b=b, c=c, real=real: e.bn_stats(stats[:, c, j, :], hid[:, b, c, 0:real]), t_ev[j])
            t_out[j] = sp.dma(lambda e, b=b, w0=w0, m=m: e.dma_start(k.hidden[:, :, w0 * P:w0 * P + m], hid[:, b, :, 0:m]), k.qv_out[b], t_ev[j])
        sp.wait(k.qv_out[0].token, k.qv_out[1].token)
        for c in range(2):
            t = dve.do(lambda e, c=c: e.bn_aggr(moments[:, c, :], stats[:, c, :, :].rearrange("p j s -> p (j s)")), t_st[len(BLOCKS) - 1])
        t = root(k, moments[:, :, 1], t)
        t = dve.do(lambda e: e.tensor_tensor(moments[:, :, 1], moments[:, :, 1], cols[:, 1, :], ALU.mult), t)
        t = dve.do(lambda e: e.tensor_tensor(moments[:, :, 0], moments[:, :, 0], moments[:, :, 1], ALU.mult), t)
        t_bn = dve.do(lambda e: e.tensor_tensor(moments[:, :, 0], cols[:, 2, :], moments[:, :, 0], ALU.subtract), t)
        run_lanes(k)

        t_z = dve.do(lambda e: e.memset(k.acc_flat[:, :], 0.0))
        t_in, t_r, t_o, t_x = ({} for _ in range(4))

        def fetch(j):
            w0, n = BLOCKS[j]
            t_in[j] = sp.dma(lambda e: e.dma_start(hid[:, j % 2, :, 0:n * P], k.hidden[:, :, w0 * P:(w0 + n) * P]), k.qv_out[2 + j % 2], *got(t_r, j - 2))
        def warm(j):
            b, m = j % 2, BLOCKS[j][1] * P
            for c in range(2):
                t_r[j] = act.do(lambda e, b=b, c=c, m=m: e.activation(hot[:, b, c, 0:m], hid[:, b, c, 0:m], ACT.Relu, bias=moments[:, c, 0:1], scale=moments[:, c, 1:2]),
                                t_in[j], t_bn, *got(t_o, j - 2))

        fetch(0)
        fetch(1)
        warm(0)
        for j, (w0, n) in enumerate(BLOCKS):
            b, m = j % 2, n * P
            if j + 1 < len(BLOCKS):
                warm(j + 1)
            if j + 2 < len(BLOCKS):
                fetch(j + 2)
            for i in range(n):
                for c in range(2):
                    pe.do(lambda e, i=i, c=c, b=b: e.matmul(k.psum[b][:, i * P:(i + 1) * P], hot[:, b, c, i * P:(i + 1) * P], w2[:, c, :], start=(c == 0), stop=False),
                          t_r[j], *got(t_x, j - 2))
                t_o[j] = pe.do(lambda e, i=i, b=b: e.matmul(k.psum[b][:, i * P:(i + 1) * P], k.ones[0:1, :], b2[:, :], start=False, stop=True))
            t_x[j] = dve.do(lambda e, w0=w0, n=n, b=b, m=m: e.tensor_tensor(k.x[:, w0:w0 + n, :], k.x[:, w0:w0 + n, :],
                            k.psum[b][:, 0:m].rearrange("p (n f) -> p n f", f=F), ALU.add), t_o[j])
            plain_table(k, sb, w0, n, [t_x[j]], state)
        sp.wait(k.x_in[0].token, k.x_in[1].token)
        run_lanes(k)


def edge_conv_end(k):
    dve, act, pe, sp, a = k.dve, k.act, k.pe, k.sp, k.a
    got = lambda d, i: [d[i]] if i in d else []
    with ExitStack() as ctx:
        sb = scratch(k, ctx)
        wc = sb("wc", [7, F])
        be = sb("be", [1, F])
        w3 = sb("w3", [P, F])
        et = sb("et", [7, 2, G4 * P])
        aggt = sb("aggt", [P, 2, G4 * P])
        out = sb("out_sb", [P, 2, G4, F])
        vec = lambda n: a[n].rearrange("(a n) -> a n", a=1)
        t_w = load_rows(k, [(wc[0:1, :], vec("L3_gnn_b")), (wc[1:7, :], a["L3_gnn_We"]), (be[:, :], vec("L3_gnn_be")), (w3[:, :], a["L3_gnn_W"])])
        t_wc = dve.do(lambda e: e.tensor_tensor(wc[0:1, :], wc[0:1, :], be[:, :], ALU.add), t_w)
        t_e, t_agg, t_o, t_x, t_out = ({} for _ in range(5))
        rows = k.out.rearrange("(w p) f -> p w f", p=P)
        for j, (w0, n) in enumerate(BLOCKS):
            b, m = j % 2, n * P
            for i in range(n):
                t = pe.do(lambda e, i=i, w0=w0, b=b: e.transpose(k.psum[b][0:7, i * P:(i + 1) * P], k.acc7[:, w0 + i, F:F + 7], k.ident[:, :]), *got(t_e, j - 2))
            t_e[j] = act.do(lambda e, b=b, m=m: e.copy(et[:, b, 0:m], k.psum[b][0:7, 0:m]), t, *got(t_o, j - 2))
            for i in range(n):
                t = pe.do(lambda e, i=i, w0=w0, b=b: e.transpose(k.psum[2 + b][:, i * P:(i + 1) * P], k.acc7[:, w0 + i, 0:F], k.ident[:, :]), *got(t_agg, j - 2))
            t_agg[j] = act.do(lambda e, b=b, m=m: e.copy(aggt[:, b, 0:m], k.psum[2 + b][:, 0:m]), t, *got(t_o, j - 2))
            for i in range(n):
                pe.do(lambda e, i=i, b=b: e.matmul(k.psum[4 + b][:, i * P:(i + 1) * P], aggt[:, b, i * P:(i + 1) * P], w3[:, :], start=True, stop=False),
                      t_agg[j], t_e[j], t_wc, *got(t_x, j - 2))
                t_o[j] = pe.do(lambda e, i=i, b=b: e.matmul(k.psum[4 + b][:, i * P:(i + 1) * P], et[:, b, i * P:(i + 1) * P], wc[:, :], start=False, stop=True))
            t_x[j] = dve.do(lambda e, w0=w0, n=n, b=b, m=m: e.scalar_tensor_tensor(
                out=out[:, b, 0:n, :], in0=k.psum[4 + b][:, 0:m].rearrange("p (n f) -> p n f", f=F), scalar=0.0,
                in1=k.x[:, w0:w0 + n, :], op0=ALU.max, op1=ALU.add), t_o[j], *got(t_out, j - 2))
            t_out[j] = sp.dma(lambda e, w0=w0, n=n, b=b: e.dma_start(rows[:, w0:w0 + n, :], out[:, b, 0:n, :]), k.x_in[b], t_x[j])
        sp.wait(k.x_in[0].token, k.x_in[1].token)
        run_lanes(k)


def dram_tables(k):
    counters = lambda name, n: [Counter(k.sem(f"s_{name}{i}")) for i in range(n)]
    k.x_in, k.qv_out, k.kept_out = counters("x_in", 2), counters("qv_out", 4), counters("kept_out", 4)
    k.t_qv, k.t_kept = {}, {}
    dram = lambda name, shape: k.nc.dram_tensor(name, shape, F32).ap()
    k.table_qv = dram("table_qv", [NP, 2 * F])
    k.table_xw = dram("table_xw", [NP * R, F])
    k.table_h = dram("table_h", [NP, F])
    k.kept = dram("kept_rows", [P, W, 2 * F])
    k.hidden = dram("hidden", [P, 2, NP])


def layers(k):
    nc = k.nc
    k.acc_flat = k.sb("acc", [P, (W + 1) * (F + 17)])
    part = lambda n: k.acc_flat[:, 0:(W + 1) * n].rearrange("p (w n) -> p w n", n=n)
    k.acc, k.acc17, k.acc7 = part(F), part(F + 17), part(F + 7)
    k.sums = part(H * (D + 1) + R)
    k.x = k.sb("x", [P, W + 1, F])
    k.keys = k.x
    k.inverse = k.sb("inverse", [P, W + 1, R])
    top = k.sb("top", [P, W + 1, H])
    k.pool.do(lambda e: e.memset(top[:, :, :], NONE))
    k.pool.do(lambda e: e.memset(k.acc_flat[:, :], 0.0))
    k.pool.do(lambda e: e.memset(k.keys[:, W, :], 0.0))
    k.sp.wait(load_rows(k, [(k.keys[:, 0:W, :], k.kept[:, :, 0:F])]))
    run_lanes(k)
    attention_pass(k, k.rec_dst, CD, k.win_dst, k.table_qv, k.keys, top, k.sums)
    count_edges(k)
    attention_to_relation(k)
    relation_pass(k, k.rec_dst, CD, k.win_dst, k.table_xw, k.acc)
    relation_pass(k, k.rec_src, CS, k.win_src, k.table_xw, k.acc)
    gine_tables(k)
    sum_pass(k, k.rec_src, CS, k.win_src, k.table_h, k.acc17, 17)
    gine_end(k)
    sum_pass(k, k.rec_dst, CD, k.win_dst, k.table_h, k.acc7, 7)
    edge_conv_end(k)


_EDGE = ("src", "dst", "edge_type_8", "edge_attr_16", "edge_attr_6")


def kernel(**inputs):
    import concourse.bacc as bacc
    from concourse.bass_utils import run_bass_kernel_spmd

    nc = bacc.Bacc("TRN2", target_bir_lowering=False, num_devices=1)
    arrays, aps = {}, {}
    for name, a in inputs.items():
        a = np.asarray(a)
        if name in _EDGE:
            fill = np.full((ET * P - E, *a.shape[1:]), N if name in ("src", "dst") else 0, a.dtype)
            a = np.concatenate([a, fill])
        if name == "x":
            a = np.concatenate([a, np.zeros((NP - N, F), a.dtype)])
        if a.ndim == 0:
            a = a.reshape(1)
        a = np.ascontiguousarray(a)
        arrays[f"in_{name}"] = a
        aps[name] = nc.dram_tensor(f"in_{name}", a.shape, mybir.dt.from_np(a.dtype), kind="ExternalInput").ap()
    out = nc.dram_tensor("out", [NP, F], F32, kind="ExternalOutput").ap()
    build_program(nc, aps, out)
    result = run_bass_kernel_spmd(nc, [arrays], core_ids=[0])
    return result.results[0]["out"][:N]
```
